# Optimizing a Trainium2 kernel written in Bass

```python
import numpy as np
import jax
import jax.numpy as jnp

def _softmax(x, axis=-1):
    return jax.nn.softmax(x, axis=axis)

def _gelu(x):
    return jax.nn.gelu(x, approximate=True)

def _silu(x):
    return jax.nn.silu(x)

def _sigmoid(x):
    return jax.nn.sigmoid(x)

def _layernorm(x, axis=-1, eps=1e-05):
    m = jnp.mean(x, axis=axis, keepdims=True)
    v = jnp.var(x, axis=axis, keepdims=True)
    return (x - m) / jnp.sqrt(v + eps)

def _scatter_add(tgt, idx, src, axis=0):
    return tgt.at[idx].add(src)

def _segment_sum(src, seg, n):
    return jax.ops.segment_sum(src, seg, n)
kernel_name = 'mk_xattn_ffn_d1_seqx_r4_4fec20'

def setup_inputs(seed: int=0):
    np.random.seed(seed)
    _w = jnp.asarray

    def _rec_inputs():
        import jax
        import jax.numpy as jnp
        _rk = jax.random.key(seed)
        x = 0.002226 + 0.9996 * jax.random.normal(jax.random.fold_in(_rk, 1), (2, 1024, 256), jnp.float32)
        _lenS = 1024 - jax.random.randint(jax.random.fold_in(_rk, 7), (2,), 0, max(1, 1024 // 4) + 1, jnp.int32)
        _lenS2 = 64 - jax.random.randint(jax.random.fold_in(_rk, 8), (2,), 0, max(1, 64 // 4) + 1, jnp.int32)
        _ctx_1024P = jax.random.normal(jax.random.fold_in(_rk, 11), (2, 16, 256), jnp.float32)
        _ctx_1024c = jax.random.dirichlet(jax.random.fold_in(_rk, 511), 0.3 * jnp.ones((16,), jnp.float32), (2, 64))
        _ctx_1024t = jnp.einsum('bsk,bkd->bsd', _ctx_1024c, _ctx_1024P)
        _ctx_1024t = _ctx_1024t * jax.lax.rsqrt(jnp.mean(jnp.square(_ctx_1024t)) + 1e-12) * 0.953939
        ctx_1024 = -7.10856e-05 + 0.999911 * (_ctx_1024t + 0.3 * jax.random.normal(jax.random.fold_in(_rk, 611), (2, 64, 256), jnp.float32))
        _validS = jnp.arange(1024)[None, :] < _lenS[:, None]
        _validS2 = jnp.arange(64)[None, :] < _lenS2[:, None]
        _causal = jnp.tril(jnp.ones((1024, 1024), dtype=bool))
        mask_BxS2_bk0 = jnp.logical_not(jnp.broadcast_to(_validS2[:, :], (2, 64)))
        return (x, ctx_1024, mask_BxS2_bk0)
    x, ctx_1024, mask_BxS2_bk0 = _rec_inputs()

    def _L0_xattn_setup():
        import jax, jax.numpy as jnp
        import numpy as np
        DIM, DIM_HEAD, HEADS, SCALE = (256, 64, 8, 8.0)
        INNER = DIM_HEAD * HEADS
        LN_EPS = 1e-05
        L2_EPS = 1e-12

        def layer_norm(x, w, b):
            mu = jnp.mean(x, axis=-1, keepdims=True)
            var = jnp.mean(jnp.square(x - mu), axis=-1, keepdims=True)
            return (x - mu) * jax.lax.rsqrt(var + LN_EPS) * w + b

        def l2norm(t):
            n = jnp.sqrt(jnp.sum(jnp.square(t), axis=-1, keepdims=True))
            return t / jnp.maximum(n, L2_EPS)
        key = jax.random.key(seed)
        ks = jax.random.split(key, 8)
        b, n, m = (8, 2048, 64)
        x = jax.random.normal(ks[0], (b, n, DIM), dtype=jnp.float32)
        latents = jax.random.normal(ks[1], (b, m, DIM), dtype=jnp.float32)
        mask = jax.random.randint(ks[2], (b, n), 0, 2) > 0
        Wq = jax.random.normal(ks[3], (DIM, INNER), dtype=jnp.float32) * DIM ** (-0.5)
        Wkv = jax.random.normal(ks[4], (DIM, 2 * INNER), dtype=jnp.float32) * DIM ** (-0.5)
        Wo = jax.random.normal(ks[5], (INNER, DIM), dtype=jnp.float32) * INNER ** (-0.5)
        return {'x': x, 'latents': latents, 'mask': mask, 'ln_x_w': jnp.ones((DIM,)), 'ln_x_b': jnp.zeros((DIM,)), 'ln_l_w': jnp.ones((DIM,)), 'ln_l_b': jnp.zeros((DIM,)), 'Wq': Wq, 'Wkv': Wkv, 'q_scale': jnp.ones((DIM_HEAD,)), 'k_scale': jnp.ones((DIM_HEAD,)), 'Wo': Wo, 'ln_o_w': jnp.ones((DIM,)), 'ln_o_b': jnp.zeros((DIM,))}
    _L0_xattn_all = _L0_xattn_setup()
    _L0_xattn_in = {k: v for k, v in _L0_xattn_all.items() if k in ('ln_x_w', 'ln_x_b', 'ln_l_w', 'ln_l_b', 'Wq', 'Wkv', 'q_scale', 'k_scale', 'Wo', 'ln_o_w', 'ln_o_b')}
    del _L0_xattn_all

    def _L0_ffn_setup():
        import jax, jax.numpy as jnp
        import numpy as np
        B, S, D = (4, 1024, 256)
        H = 1024
        RH = 256
        E = 16
        K = 2
        NS = 1

        def _swiglu(x, w1, w2, w3):
            return jax.nn.silu(x @ w1) * (x @ w2) @ w3
        key = jax.random.key(seed)
        ks = jax.random.split(key, 9)
        s = 0.02
        return {'x': jax.random.normal(ks[0], (B, S, D), dtype=jnp.float32), 'router_w': jax.random.normal(ks[1], (D, E), dtype=jnp.float32) * s, 'expert_bias': jnp.zeros((E,), dtype=jnp.float32), 'shared_w1': jax.random.normal(ks[2], (NS, D, H), dtype=jnp.float32) * s, 'shared_w2': jax.random.normal(ks[3], (NS, D, H), dtype=jnp.float32) * s, 'shared_w3': jax.random.normal(ks[4], (NS, H, D), dtype=jnp.float32) * s, 'routed_w1': jax.random.normal(ks[5], (E, D, RH), dtype=jnp.float32) * s, 'routed_w2': jax.random.normal(ks[6], (E, D, RH), dtype=jnp.float32) * s, 'routed_w3': jax.random.normal(ks[7], (E, RH, D), dtype=jnp.float32) * s}
    _L0_ffn_all = _L0_ffn_setup()
    _L0_ffn_in = {k: v for k, v in _L0_ffn_all.items() if k in ('router_w', 'expert_bias', 'shared_w1', 'shared_w2', 'shared_w3', 'routed_w1', 'routed_w2', 'routed_w3')}
    del _L0_ffn_all
    return {'x': x, 'ctx_1024': ctx_1024, 'mask_BxS2_bk0': mask_BxS2_bk0, 'L0_xattn_ln_x_w': _L0_xattn_in['ln_x_w'], 'L0_xattn_ln_x_b': _L0_xattn_in['ln_x_b'], 'L0_xattn_ln_l_w': _L0_xattn_in['ln_l_w'], 'L0_xattn_ln_l_b': _L0_xattn_in['ln_l_b'], 'L0_xattn_Wq': _L0_xattn_in['Wq'], 'L0_xattn_Wkv': _L0_xattn_in['Wkv'], 'L0_xattn_q_scale': _L0_xattn_in['q_scale'], 'L0_xattn_k_scale': _L0_xattn_in['k_scale'], 'L0_xattn_Wo': _L0_xattn_in['Wo'], 'L0_xattn_ln_o_w': _L0_xattn_in['ln_o_w'], 'L0_xattn_ln_o_b': _L0_xattn_in['ln_o_b'], 'L0_ffn_router_w': _L0_ffn_in['router_w'], 'L0_ffn_expert_bias': _L0_ffn_in['expert_bias'], 'L0_ffn_shared_w1': _L0_ffn_in['shared_w1'], 'L0_ffn_shared_w2': _L0_ffn_in['shared_w2'], 'L0_ffn_shared_w3': _L0_ffn_in['shared_w3'], 'L0_ffn_routed_w1': _L0_ffn_in['routed_w1'], 'L0_ffn_routed_w2': _L0_ffn_in['routed_w2'], 'L0_ffn_routed_w3': _L0_ffn_in['routed_w3']}

def reference(x, ctx_1024, mask_BxS2_bk0, L0_xattn_ln_x_w, L0_xattn_ln_x_b, L0_xattn_ln_l_w, L0_xattn_ln_l_b, L0_xattn_Wq, L0_xattn_Wkv, L0_xattn_q_scale, L0_xattn_k_scale, L0_xattn_Wo, L0_xattn_ln_o_w, L0_xattn_ln_o_b, L0_ffn_router_w, L0_ffn_expert_bias, L0_ffn_shared_w1, L0_ffn_shared_w2, L0_ffn_shared_w3, L0_ffn_routed_w1, L0_ffn_routed_w2, L0_ffn_routed_w3):
    import jax
    import jax.numpy as jnp

    def _L0_xattn_ref(x, latents, mask, ln_x_w, ln_x_b, ln_l_w, ln_l_b, Wq, Wkv, q_scale, k_scale, Wo, ln_o_w, ln_o_b):
        import jax, jax.numpy as jnp
        import numpy as np
        DIM, DIM_HEAD, HEADS, SCALE = (256, 64, 8, 8.0)
        INNER = DIM_HEAD * HEADS
        LN_EPS = 1e-05
        L2_EPS = 1e-12

        def layer_norm(x, w, b):
            mu = jnp.mean(x, axis=-1, keepdims=True)
            var = jnp.mean(jnp.square(x - mu), axis=-1, keepdims=True)
            return (x - mu) * jax.lax.rsqrt(var + LN_EPS) * w + b

        def l2norm(t):
            n = jnp.sqrt(jnp.sum(jnp.square(t), axis=-1, keepdims=True))
            return t / jnp.maximum(n, L2_EPS)
        b, n, _ = x.shape
        m = latents.shape[1]
        x = layer_norm(x, ln_x_w, ln_x_b)
        latents = layer_norm(latents, ln_l_w, ln_l_b)
        q = latents @ Wq
        kv_input = jnp.concatenate([x, latents], axis=1)
        kv = kv_input @ Wkv
        k, v = jnp.split(kv, 2, axis=-1)

        def to_heads(t):
            return t.reshape(t.shape[0], t.shape[1], HEADS, DIM_HEAD).transpose(0, 2, 1, 3)
        q, k, v = map(to_heads, (q, k, v))
        q = l2norm(q) * q_scale
        k = l2norm(k) * k_scale
        sim = jnp.einsum('bhid,bhjd->bhij', q, k) * SCALE
        full_mask = jnp.concatenate([mask, jnp.ones((b, m), dtype=bool)], axis=1)[:, None, None, :]
        max_neg = -jnp.finfo(sim.dtype).max
        sim = jnp.where(full_mask, sim, max_neg)
        attn = jax.nn.softmax(sim.astype(jnp.float32), axis=-1).astype(sim.dtype)
        out = jnp.einsum('bhij,bhjd->bhid', attn, v)
        out = out.transpose(0, 2, 1, 3).reshape(b, m, INNER)
        return layer_norm(out @ Wo, ln_o_w, ln_o_b)

    def _L0_ffn_ref(x, router_w, expert_bias, shared_w1, shared_w2, shared_w3, routed_w1, routed_w2, routed_w3):
        import jax, jax.numpy as jnp
        import numpy as np
        B, S, D = (4, 1024, 256)
        H = 1024
        RH = 256
        E = 16
        K = 2
        NS = 1

        def _swiglu(x, w1, w2, w3):
            return jax.nn.silu(x @ w1) * (x @ w2) @ w3
        shared_out = jnp.sum(jax.vmap(lambda w1, w2, w3: _swiglu(x, w1, w2, w3))(shared_w1, shared_w2, shared_w3), axis=0)
        scores = jax.nn.sigmoid(x @ router_w)
        sel_scores = scores + expert_bias
        _, top_idx = jax.lax.top_k(sel_scores, K)
        top_scores = jnp.take_along_axis(scores, top_idx, axis=-1)
        gates = jnp.sum(jax.nn.one_hot(top_idx, E, dtype=scores.dtype) * top_scores[..., None], axis=-2)
        xf = x.reshape(-1, D)
        gf = gates.reshape(-1, E).T

        def body(acc, ws):
            w1, w2, w3, g = ws
            return (acc + _swiglu(xf, w1, w2, w3) * g[:, None], None)
        routed_out, _ = jax.lax.scan(body, jnp.zeros_like(xf), (routed_w1, routed_w2, routed_w3, gf))
        return shared_out + routed_out.reshape(x.shape)
    x = x + _L0_xattn_ref(ctx_1024, _layernorm(x, axis=-1), mask_BxS2_bk0, L0_xattn_ln_x_w, L0_xattn_ln_x_b, L0_xattn_ln_l_w, L0_xattn_ln_l_b, L0_xattn_Wq, L0_xattn_Wkv, L0_xattn_q_scale, L0_xattn_k_scale, L0_xattn_Wo, L0_xattn_ln_o_w, L0_xattn_ln_o_b)
    x = x + _L0_ffn_ref(_layernorm(x, axis=-1), L0_ffn_router_w, L0_ffn_expert_bias, L0_ffn_shared_w1, L0_ffn_shared_w2, L0_ffn_shared_w3, L0_ffn_routed_w1, L0_ffn_routed_w2, L0_ffn_routed_w3)
    return x

_drawn_inputs = setup_inputs


def setup_inputs(seed=0):
    import zlib

    import numpy as np

    out = dict(_drawn_inputs(seed))
    spreads = {'L0_xattn_ln_x_w': (1.0, 0.6),
     'L0_xattn_ln_x_b': (0.0, 0.732),
     'L0_xattn_ln_l_w': (1.0, 0.2),
     'L0_xattn_ln_l_b': (0.0, 0.1),
     'L0_xattn_q_scale': (1.0, 0.2),
     'L0_xattn_k_scale': (1.0, 0.2),
     'L0_xattn_ln_o_w': (1.0, 0.2),
     'L0_xattn_ln_o_b': (0.0, 0.1),
     'L0_ffn_expert_bias': (0.0, 0.731)}
    factors = {'L0_ffn_router_w': 8.0,
     'L0_ffn_routed_w1': 6.155,
     'L0_ffn_routed_w2': 6.117,
     'L0_ffn_routed_w3': 6.101,
     'L0_ffn_shared_w1': 7.347,
     'L0_ffn_shared_w2': 7.323,
     'L0_ffn_shared_w3': 7.319}
    for name, (base, spread) in spreads.items():
        noise = np.random.default_rng([zlib.crc32(name.encode()), seed]).standard_normal(out[name].shape)
        drawn = base * np.exp(spread * noise) if base else spread * noise
        out[name] = jnp.asarray(drawn.astype(out[name].dtype))
    for name, factor in factors.items():
        out[name] = (out[name] * factor).astype(out[name].dtype)
    return out
```

```python
from contextlib import ExitStack

import concourse.bass as bass
from concourse import mybir

F32 = mybir.dt.float32
F32R = mybir.dt.float32r
I32 = mybir.dt.int32
ACT = mybir.ActivationFunctionType
ALU = mybir.AluOpType
AX = mybir.AxisListType

B, S, D = 2, 1024, 256
M = 64
H, DH = 8, 64
INNER = H * DH
P = 128
DK = D // P
TQ = S // P
TK = TQ + 1
NT = B * TQ
BH = B * H
QC = 512
CH = S // QC
STEPS = CH * TK
SCALE = 8.0
LN_EPS, L2_EPS = 1e-5, 1e-12
MASKED = -1e30
E, HID = 16, 256
SH = 1024
SU = SH // P
GR = 512
NG = NT * P // GR
TOP = 2
NS = (TOP * NT * P + E * (P - 1)) // P
FAR = 99.0
KEYS = S + M
PIECES = [(0, 384), (384, 384), (768, KEYS - 768)]
NP_ = len(PIECES) * TQ


def wait(eng, sem, value):
    if isinstance(value, int) and value <= 0:
        return
    eng.wait_ge(sem, value)


def build(nc, x, ctx, mask, ln_x_w, ln_x_b, ln_l_w, ln_l_b, wq, wkv, q_scale, k_scale, wo,
          ln_o_w, ln_o_b, router_w, expert_bias, sw1, sw2, sw3, rw1, rw2, rw3, out, dbg=None):
    es = ExitStack()

    def sb(name, shape, dt=F32, stack=es):
        return stack.enter_context(nc.sbuf_tensor(name, shape, dt))

    def sem(name):
        return es.enter_context(nc.semaphore(name))

    xs_dram = nc.dram_tensor("slot_rows", (NS * P, D), F32, kind="Internal").ap()
    ys_dram = nc.dram_tensor("slot_results", (NS * P, D), F32, kind="Internal").ap()

    ident = sb("ident", [P, P])
    eps = sb("eps", [P, 1])
    zero = sb("zero", [P, 1])
    zrow = sb("zrow", [P, D])
    lnw = sb("lnw", [P, 2, 2, DK])
    qks = sb("qks", [P, 2])
    maskf = sb("maskf", [P, BH])
    maskrow = sb("maskrow", [P, BH, M])
    mask_i = sb("mask_i", [M, B], I32)
    maskrow_i = sb("maskrow_i", [1, B, M], I32)
    firstrow = sb("firstrow", [P, P])
    wr = sb("wr", [P, DK, E])
    ebias = sb("ebias", [P, E])
    exps = sb("exps", [P, NS + 1], I32)
    posi = sb("posi", [P, NT, TOP], I32)
    gate = sb("gate", [P, NT, TOP])
    logits = sb("logits", [P, NT, E])
    st = sb("st", [P, 2, 6])
    mv = sb("mv", [P, 2, 2])
    sd = sb("sd", [P, 2, 1])
    rs = sb("rs", [P, 2, 1])

    att = ExitStack()
    on = sb("on", [P, BH, TQ, DH], stack=att)
    kn = sb("kn", [P, BH, TK, DH], stack=att)
    vn = sb("vn", [P, BH, TK, DH + 1], stack=att)
    wqkv = sb("wqkv", [P, DK, 3 * INNER], stack=att)
    xin = sb("xin", [P, 2, D], stack=att)
    xn = sb("xn", [P, 2, D], stack=att)
    xn2 = sb("xn2", [P, 2, D], stack=att)
    xT = sb("xT", [P, 2, DK, P], stack=att)
    sq = sb("sq", [P, 2, INNER], stack=att)
    ssq = sb("ssq", [P, 2 * H], stack=att)
    nrm = sb("nrm", [P, 2 * H], stack=att)
    rnr = sb("rnr", [P, 2 * H], stack=att)
    dup = sb("dup", [P, TQ + TK, 2, DH], stack=att)
    qT1 = [sb(f"q_hi_lo{i}", [P, S], F32R, att) for i in range(2)]
    qT2 = [sb(f"q_hi_max{i}", [P, S], F32R, att) for i in range(2)]
    kT1 = [sb(f"k_hi_hi{i}", [P, TK * P], F32R, att) for i in range(2)]
    kT2 = [sb(f"k_lo_one{i}", [P, TK * P], F32R, att) for i in range(2)]
    prob = sb("prob", [P, 3, QC], stack=att)
    mx = sb("mx", [P, TQ, len(PIECES)], stack=att)
    mbias = [sb(f"mbias{i}", [P, 1], stack=att) for i in range(2)]
    mm = sb("mm", [P, TQ], stack=att)
    zneg = sb("zneg", [P, TQ, DH + 1], stack=att)
    rec = sb("rec", [P, 2, QC // P], stack=att)
    att.close()

    ffn = ExitStack()
    w3r = sb("w3r", [P, E, HID // P, D], stack=ffn)
    x2 = sb("x2", [P, NT, D], stack=ffn)
    xf = sb("xf", [P, NT, D], stack=ffn)
    xfT = sb("xfT", [P, DK, NT * P], stack=ffn)
    w12r = sb("w12r", [P, E, DK, 2 * HID], stack=ffn)
    w12s = sb("w12s", [P, DK, 2, SH], stack=ffn)
    w3s = sb("w3s", [P, SU, D], stack=ffn)

    gat = [sb(f"slot_result{i}", [P, TOP, D], stack=ffn) for i in range(4)]

    cst = ExitStack()
    wo_sb = sb("wo_sb", [P, INNER // P, D], stack=cst)
    lno = sb("lno", [P, 2, D], stack=cst)
    xres = sb("xres", [P, 2, D], stack=cst)
    obuf = sb("obuf", [P, 2, INNER], stack=cst)
    oT = sb("oT", [P, 2, INNER], stack=cst)
    yn = sb("yn", [P, 2, D], stack=cst)
    xfb = sb("xfb", [P, 2, DK, P], stack=cst)
    cst.close()

    moe = ExitStack()
    sil = sb("sil", [P, 2, GR], stack=moe)
    gsh = sb("gsh", [P, 2, GR], stack=moe)
    xsl = sb("xsl", [P, 4, D], stack=moe)
    xsT = sb("xsT", [P, 2, DK, P], stack=moe)
    rg = sb("rg", [P, 2, HID], stack=moe)
    rgT = sb("rgT", [P, 2, HID], stack=moe)
    yo = sb("yo", [P, 2, D], stack=moe)
    moe.close()
    ffn.close()
    rt = ExitStack()
    rt.enter_context(nc.sbuf_tensor("below_routing", [P, (B * H * TQ * DH) + 3 * NT * D], F32))
    onehot = [sb(f"onehot{k}", [P, NT, E], stack=rt) for k in range(TOP)]
    score = sb("score", [P, NT, E], stack=rt)
    sel = sb("sel", [P, NT, E], stack=rt)
    work = [sb(f"work{k}", [P, NT, E], stack=rt) for k in range(2)]
    best = sb("best", [P, NT], stack=rt)
    number = sb("number", [P, E], stack=rt)
    number_i = sb("number_i", [P, E], I32, rt)
    slot_i = sb("slot_i", [1, NS + 1], I32, rt)
    slot_f = sb("slot_f", [1, NS + 1], stack=rt)
    passed = sb("passed", [1, NS + 1, E], stack=rt)
    passed_sum = sb("passed_sum", [1, NS + 1], stack=rt)
    upper = sb("upper", [P, P], stack=rt)
    allones = sb("allones", [P, P], stack=rt)
    taken = sb("taken", [P, E], stack=rt)
    tiles_i = sb("tiles_i", [P, E], I32, rt)
    tiles_f = sb("tiles_f", [P, E], stack=rt)
    ends = [sb(f"ends{k}", [P, E], stack=rt) for k in range(2)]
    offs = sb("offs", [P, E], stack=rt)
    posf = sb("posf", [P, NT], stack=rt)
    rt.close()

    bank = [es.enter_context(nc.psum_tensor(f"bank{i}", [P, 512], F32)) for i in range(8)]

    consts_loaded, consts_made, masks_made = sem("consts_loaded"), sem("consts_made"), sem("masks_made")
    zeros_made, xs_zeroed = sem("zeros_made"), sem("xs_zeroed")
    x_loaded, x_used, var_ready, sd_ready = sem("x_loaded"), sem("x_used"), sem("var_ready"), sem("sd_ready")
    xnorm_ready, xt_turned, xT_ready = sem("xnorm_ready"), sem("xt_turned"), sem("xT_ready")
    q_made, k_made, v_made = sem("q_made"), sem("k_made"), sem("v_made")
    sq_ready, ssq_ready, nrm_ready = sem("sq_ready"), sem("ssq_ready"), sem("nrm_ready")
    q_used, k_used, v_used = sem("q_used"), sem("k_used"), sem("v_used")
    dup_ready, heads_turned, scaled, split = sem("dup_ready"), sem("heads_turned"), sem("scaled"), sem("split")
    piece_made, piece_used = sem("piece_made"), sem("piece_used")
    neg_ready, neg_turned, neg_row = sem("neg_ready"), sem("neg_turned"), sem("neg_row")
    scores_made, probs_ready, pv_done = sem("scores_made"), sem("probs_ready"), sem("pv_done")
    o_ready = sem("o_ready")
    c_loaded, xres_loaded, xres_ready, xres_used = sem("c_loaded"), sem("xres_loaded"), sem("xres_ready"), sem("xres_used")
    ob_ready, o_turned, oT_ready = sem("ob_ready"), sem("o_turned"), sem("oT_ready")
    y_made, y_used, cvar_ready, csd_ready = sem("y_made"), sem("y_used"), sem("cvar_ready"), sem("csd_ready")
    xf_ready, xf_kept, xf_turned, xf_stat, xf_moved = (sem("xf_ready"), sem("xf_kept"), sem("xf_turned"),
                                                     sem("xf_stationary"), sem("xf_moving"))
    logits_made, logits_ready = sem("logits_made"), sem("logits_ready")
    d_consts, score_ready, taken_ready, counts_made, routed = (sem("d_consts"), sem("score_ready"),
                                                              sem("taken_ready"), sem("counts_made"), sem("routed"))
    scattered = sem("scattered")
    ws_loaded, wr_loaded = sem("shared_weights_loaded"), sem("routed_weights_loaded")
    hid_made, sil_ready, hid_ready, ysh_made, ysh_added = (sem("hid_made"), sem("sil_ready"), sem("hid_ready"),
                                                         sem("ysh_made"), sem("ysh_added"))
    slot_loaded = [sem(f"slot_loaded{i}") for i in range(4)]
    slot_turned, slotT_ready, rh_made, rsil_ready, rg_ready = (sem("slot_turned"), sem("slotT_ready"),
                                                             sem("rh_made"), sem("rsil_ready"), sem("rg_ready"))
    rg_turned, rgT_ready, ry_made, yo_ready = sem("rg_turned"), sem("rgT_ready"), sem("ry_made"), sem("yo_ready")
    yo_stored = [sem(f"yo_stored{i}") for i in range(2)]
    gathered = [sem(f"gathered{i}") for i in range(4)]
    combined, out_stored = sem("combined"), sem("out_stored")

    NC_CONST = 20

    def pair_loop(eng, body, n):
        body(0)
        with eng.Fori(1, n - 1) as t:
            body(t)
        body(n - 1)

    def head_loop(eng, body):
        body(0, 0, True)
        body(1, 1, True)
        with eng.Fori(1, BH // 2 - 1) as i:
            body(2 * i, 0, True)
            body(2 * i + 1, 1, True)
        body(BH - 2, 0, True)
        body(BH - 1, 1, False)

    def inside(s):
        return not isinstance(s, int) or 0 <= s < NS

    def slot_loop(eng, body):
        for c in range(4):
            body(c, 0, c)
        with eng.Fori(1, NS // 4) as i:
            for c in range(4):
                body(4 * i + c, i, c)
        for s in range(NS // 4 * 4, NS + 2):
            body(s, s // 4, s % 4)

    piece_steps, at = {}, 0
    for s in range(5, 16):
        n = 3 if s >= 14 else 2
        piece_steps[s] = range(at, at + n)
        at += n
    assert at == NP_
    TURNS = [("k", 0, 4), ("k", 4, 4), ("k", 8, 1), ("q", 0, 4), ("q", 4, 4)]
    NTURN = len(TURNS)
    TURN_BANK = [6, 7, 6, 7, 6]
    NEG_BANK = [7, 6]

    block = es.enter_context(nc.Block())

    @block.sync
    def _(sp):
        c = consts_loaded
        for kind, vecs in enumerate(((ln_l_w, ln_l_b), (ln_x_w, ln_x_b))):
            for i, vec in enumerate(vecs):
                for k in range(DK):
                    sp.dma_start(lnw[:, kind, i, k:k + 1],
                                 vec[k * P:(k + 1) * P].rearrange("(p a) -> p a", a=1)).then_inc(c, 16)

        def load_x(t, kind):
            wait(sp, x_used, t)
            for b in range(B):
                if kind == "latent":
                    sp.dma_start(xin[:, b, :], x[b, bass.ds(t * P, P), :]).then_inc(x_loaded, 16)
                else:
                    for r in range(P // M):
                        sp.dma_start(xin[r * M:(r + 1) * M, b, :], ctx[b, :, :]).then_inc(x_loaded, 16)

        load_x(0, "latent")
        for k in range(DK):
            sp.dma_start(wqkv[:, k, 0:INNER], wq[k * P:(k + 1) * P, :]).then_inc(c, 16)
            sp.dma_start(wqkv[:, k, INNER:], wkv[k * P:(k + 1) * P, :]).then_inc(c, 16)
        for r in range(2):
            sp.dma_start(qks[r * DH:(r + 1) * DH, 0:1], q_scale.rearrange("(p a) -> p a", a=1)).then_inc(c, 16)
            sp.dma_start(qks[r * DH:(r + 1) * DH, 1:2], k_scale.rearrange("(p a) -> p a", a=1)).then_inc(c, 16)
        for b in range(B):
            sp.dma_start(mask_i[:, b:b + 1], mask[b, :].rearrange("(m a) -> m a", a=1)).then_inc(c, 16)
        sp.dma_start(maskrow_i[:, :, :], mask.rearrange("(a b) m -> a b m", a=1)).then_inc(c, 16)
        sp.dma_start(wr[:, :, :], router_w.rearrange("(k p) e -> p k e", p=P)).then_inc(c, 16)
        with sp.Fori(1, TQ) as t:
            load_x(t, "latent")
        load_x(TQ, "context")

        sp.wait_ge(zeros_made, 1)
        for s in range(NS):
            sp.dma_start(xs_dram[s * P:(s + 1) * P, :], zrow[:, :]).then_inc(xs_zeroed, 16)

        sp.wait_ge(o_ready, CH * BH)
        sp.wait_ge(scaled, NTURN * BH)
        sp.dma_start(wo_sb[:, :, :], wo.rearrange("(k p) d -> p k d", p=P)).then_inc(c_loaded, 16)
        sp.dma_start(lno[:, 0, :], ln_o_w.rearrange("(a d) -> a d", a=1).to_broadcast([P, D])).then_inc(c_loaded, 16)
        sp.dma_start(lno[:, 1, :], ln_o_b.rearrange("(a d) -> a d", a=1).to_broadcast([P, D])).then_inc(c_loaded, 16)
        sp.dma_start(ebias[:, :], expert_bias.rearrange("(a d) -> a d", a=1).to_broadcast([P, E])).then_inc(c_loaded, 16)

        def load_res(t):
            wait(sp, xres_used, t)
            for b in range(B):
                sp.dma_start(xres[:, b, :], x[b, bass.ds(t * P, P), :]).then_inc(xres_loaded, 16)

        load_res(0)
        for w, src in enumerate((sw1, sw2)):
            sp.dma_start(w12s[:, :, w, :], src[0].rearrange("(k p) h -> p k h", p=P)).then_inc(ws_loaded, 16)
        sp.dma_start(w3s[:, :, :], sw3[0].rearrange("(u p) d -> p u d", p=P)).then_inc(ws_loaded, 16)
        with sp.Fori(1, TQ) as t:
            load_res(t)
        sp.wait_ge(routed, 1)
        with sp.Fori(0, E) as e:
            sp.dma_start(w12r[:, e, :, 0:HID], rw1[e].rearrange("(k p) h -> p k h", p=P)).then_inc(wr_loaded, 16)
            sp.dma_start(w12r[:, e, :, HID:], rw2[e].rearrange("(k p) h -> p k h", p=P)).then_inc(wr_loaded, 16)
            sp.dma_start(w3r[:, e, :, :], rw3[e].rearrange("(k p) d -> p k d", p=P)).then_inc(wr_loaded, 16)

        sp.wait_ge(scattered, 16 * NT * TOP)

        def slot(s, i, c):
            if inside(s + 3):
                wait(sp, slot_turned, s)
                sp.dma_start(xsl[:, (c + 3) % 4, :], xs_dram[bass.ds((s + 3) * P, P), :])\
                    .then_inc(slot_loaded[(c + 3) % 4], 16)
            if inside(s - 2):
                sp.wait_ge(yo_ready, s - 1)
                sp.dma_start(ys_dram[bass.ds((s - 2) * P, P), :], yo[:, c % 2, :]).then_inc(yo_stored[c % 2], 16)

        for s in range(3):
            sp.dma_start(xsl[:, s, :], xs_dram[s * P:(s + 1) * P, :]).then_inc(slot_loaded[s], 16)
        slot_loop(sp, slot)

        for n in range(NT):
            sp.wait_ge(combined, n + 1)
            sp.dma_start(out[n % B, (n // B) * P:(n // B + 1) * P, :], x2[:, n, :]).then_inc(out_stored, 16)
        sp.wait_ge(out_stored, 16 * NT)

    @block.gpsimd
    def _(pool):
        g = nc.gpsimd
        g.memset(ident[:, :], 0.0)
        g.memset(firstrow[:, :], 0.0)
        g.memset(maskrow[:, :, :], 0.0)
        g.memset(maskf[:, :], MASKED)
        g.memset(eps[:, :], LN_EPS)
        g.memset(zero[:, :], 0.0)
        g.memset(zrow[:, :], 0.0)
        g.memset(zneg[:, :, :], 0.0)
        g.memset(vn[:, :, :, DH:DH + 1], 1.0)
        g.drain()
        for i in range(2):
            g.memset(qT2[i][DH:P, :].bitcast(F32), 0.0)
            g.memset(kT2[i][DH:P, :].bitcast(F32), 0.0)
        g.drain()
        g.affine_select(out=ident[:, :], in_=ident[:, :], compare_op=ALU.not_equal, fill=1.0,
                        base=0, pattern=[[-1, P]], channel_multiplier=1)
        g.drain()
        g.memset(firstrow[0:1, :], 1.0)
        g.drain()
        for i in range(2):
            last = g.memset(kT2[i][DH:DH + 1, :].bitcast(F32), 1.0)
        last.then_inc(consts_made, 1)
        g.drain().then_inc(zeros_made, 1)
        pool.wait_ge(consts_loaded, 16 * NC_CONST)
        for b in range(B):
            for h in range(H):
                g.tensor_scalar(maskf[0:M, b * H + h:b * H + h + 1], mask_i[:, b:b + 1], -1.0, -MASKED,
                                ALU.add, ALU.mult)
                g.tensor_scalar(maskrow[0:1, b * H + h, :], maskrow_i[:, b, :], -1.0, -MASKED,
                                ALU.add, ALU.mult)
        g.tensor_scalar(qks[:, 0:1], qks[:, 0:1], SCALE, None, ALU.mult)
        g.drain().then_inc(masks_made, 1)

        pool.wait_ge(q_used, NT)
        pool.wait_ge(k_used, NT + B)

        def duplicate(hh):
            wait(pool, heads_turned, NTURN * hh)
            kin = kn[:, hh, :, :].unsqueeze(2).to_broadcast([P, TK, 2, DH])
            qin = on[:, hh, :, :].unsqueeze(2).to_broadcast([P, TQ, 2, DH])
            g.tensor_copy(dup[:, TQ:, :, :], kin)
            g.tensor_copy(dup[:, 0:TQ, :, :], qin).then_inc(dup_ready, 1)

        duplicate(0)
        with pool.Fori(1, BH) as hh:
            duplicate(hh)

        pool.wait_ge(c_loaded, 64)

        def rows_c(t):
            pool.wait_ge(xres_loaded, 32 * (t + 1))
            g.tensor_tensor(xres[:, :, :], xres[:, :, :], lno[:, 1, :].unsqueeze(1).to_broadcast([P, 2, D]),
                            ALU.add).then_inc(xres_ready, 1)
            pool.wait_ge(xf_ready, t + 1)
            g.tensor_copy(xf[:, bass.ds(2 * t, 2), :], yn[:, :, :]).then_inc(xf_kept, 1)

        with pool.Fori(0, TQ) as t:
            rows_c(t)

        g.memset(upper[:, :], 1.0)
        g.memset(allones[:, :], 1.0)
        g.iota(number_i[:, :], pattern=[[1, E]], base=-int(FAR), channel_multiplier=0)
        g.iota(slot_i[:, :], pattern=[[1, NS + 1]], base=0, channel_multiplier=0)
        g.drain()
        g.tensor_copy(number[:, :], number_i[:, :])
        g.tensor_copy(slot_f[:, :], slot_i[:, :])
        g.affine_select(out=upper[:, :], in_=upper[:, :], compare_op=ALU.is_gt, fill=0.0,
                        base=0, pattern=[[1, P]], channel_multiplier=-1)
        g.drain().then_inc(d_consts, 1)

        pool.wait_ge(routed, 1)
        pool.wait_ge(xs_zeroed, 16 * NS)
        for n in range(NT):
            for k in range(TOP):
                g.indirect_dma_start(out=xs_dram, out_offset=bass.IndirectOffsetOnAxis(ap=posi[:, n, k:k + 1], axis=0),
                                     in_=xf[:, n, :], in_offset=None).then_inc(scattered, 16)

        for p in range(2):
            pool.wait_ge(yo_stored[p], 16 * ((NS + 1 - p) // 2))
        for n in range(NT):
            wait(pool, combined, n - 3)
            for k in range(TOP):
                g.indirect_dma_start(out=gat[n % 4][:, k, :], out_offset=None, in_=ys_dram,
                                     in_offset=bass.IndirectOffsetOnAxis(ap=posi[:, n, k:k + 1], axis=0)
                                     ).then_inc(gathered[n % 4], 16)

    @block.tensor
    def _(pe):
        mm_ = nc.tensor.matmul
        pe.wait_ge(consts_made, 1)
        pe.wait_ge(consts_loaded, 16 * NC_CONST)

        def turn_x(t, c, n):
            pe.wait_ge(xnorm_ready, t + 1)
            for k in range(DK):
                last = nc.tensor.transpose(bank[c][:, k * P:(k + 1) * P], xn2[:, c, k * P:(k + 1) * P], ident[:, :])
            last.then_inc(xt_turned, 1)

        def project(n, c, latent):
            pe.wait_ge(xT_ready, n + 1)
            for j, (made, used) in enumerate(((q_made, q_used), (k_made, k_used), (v_made, v_used))):
                if j == 0 and not latent:
                    continue
                wait(pe, used, n - 1)
                for k in range(DK):
                    last = mm_(bank[2 + 3 * c + j][:, :], xT[:, c, k, :], wqkv[:, k, j * INNER:(j + 1) * INNER],
                               start=(k == 0), stop=(k == DK - 1))
                last.then_inc(made, 1)

        for c in range(B):
            turn_x(0, c, c)

        def stage_a(t):
            for c in range(B):
                project(2 * t + c, c, True)
                turn_x(t + 1, c, 2 * t + 2 + c)

        pair_loop(pe, stage_a, TQ)
        for c in range(B):
            project(NT + c, c, False)

        pe.wait_ge(q_used, NT)
        pe.wait_ge(k_used, NT + B)
        pe.wait_ge(v_used, NT + B)
        pe.wait_ge(masks_made, 1)

        def turn_head(hh, g):
            what, first, n = TURNS[g]
            if g == 0:
                pe.wait_ge(dup_ready, hh + 1)
                wait(pe, neg_row, 2 * hh)
            elif g == 1:
                wait(pe, neg_row, 2 * hh - 1)
            else:
                pe.wait_ge(split, NTURN * hh + g - 1)
            first += TQ if what == "k" else 0
            for j in range(n):
                last = nc.tensor.transpose(bank[TURN_BANK[g]][:, j * P:(j + 1) * P],
                                           dup[:, first + j, :, :].rearrange("p a d -> p (a d)"), ident[:, :])
            last.then_inc(heads_turned, 1)

        def piece(hh, p, k):
            tile, c = divmod(k, len(PIECES))
            first, n = PIECES[c]
            if k == 0:
                pe.wait_ge(split, NTURN * hh + 4)
            if tile == TQ // 2 and c == 0:
                pe.wait_ge(split, NTURN * hh + 5)
            wait(pe, piece_used, NP_ * hh + k - 1)
            dst = bank[2 + k % 2]
            last = mm_(dst[:, 0:n], qT1[p][:, tile * P:(tile + 1) * P], kT1[p][:, first:first + n],
                       start=True, stop=(c < 2))
            if c == 2:
                last = mm_(dst[:, n - M:n], firstrow[:, :], maskrow[:, hh, :], start=False, stop=True)
            last.then_inc(piece_made, 1)

        def turn_neg(hh, p):
            pe.wait_ge(neg_ready, hh + 1)
            for z in range(2):
                pe.wait_ge(split, NTURN * hh + (4 if z == 0 else 5))
                for j in range(4):
                    last = nc.tensor.transpose(bank[NEG_BANK[z]][0:DH + 1, j * P:(j + 1) * P],
                                               zneg[:, 4 * z + j, :], ident[:, :])
                last.then_inc(neg_turned, 1)

        def score_tile(hh, p, s):
            c, kt = divmod(s, TK)
            if s == 0:
                pe.wait_ge(neg_row, 2 * hh + 1)
            if s == TK:
                pe.wait_ge(neg_row, 2 * hh + 2)
            if s >= 2:
                pe.wait_ge(probs_ready, STEPS * hh + s - 1)
            mm_(bank[s % 2][:, :], kT1[p][:, kt * P:(kt + 1) * P], qT1[p][:, c * QC:(c + 1) * QC],
                start=True, stop=False)
            mm_(bank[s % 2][:, :], kT2[p][:, kt * P:(kt + 1) * P], qT2[p][:, c * QC:(c + 1) * QC],
                start=False, stop=True).then_inc(scores_made, 1)

        def weigh(hh, s):
            c, kt = divmod(s, TK)
            pe.wait_ge(probs_ready, STEPS * hh + s + 1)
            if kt == 0:
                wait(pe, o_ready, CH * hh + c - 1)
            for j in range(QC // P):
                last = mm_(bank[4 + c][:, j * (DH + 1):(j + 1) * (DH + 1)], prob[:, s % 3, j * P:(j + 1) * P],
                           vn[:, hh, kt, :], start=(kt == 0 and j == 0), stop=(kt == TK - 1),
                           skip_group_check=True)
            last.then_inc(pv_done, 1)

        for g in range(NTURN):
            turn_head(0, g)
        for k in range(NP_):
            piece(0, 0, k)
        turn_neg(0, 0)

        def stage_b(hh, p, prepare):
            for s in range(STEPS):
                score_tile(hh, p, s)
                if prepare and s < NTURN:
                    turn_head(hh + 1, s)
                if prepare:
                    for k in piece_steps.get(s, ()):
                        piece(hh + 1, 1 - p, k)
                if s:
                    weigh(hh, s - 1)
            if prepare:
                turn_neg(hh + 1, 1 - p)
            weigh(hh, STEPS - 1)

        head_loop(pe, stage_b)

        pe.wait_ge(o_ready, CH * BH)
        pe.wait_ge(c_loaded, 64)

        def out_projection(t):
            pe.wait_ge(ob_ready, t + 1)
            for c in range(B):
                for j in range(4):
                    last = nc.tensor.transpose(bank[c][:, j * P:(j + 1) * P],
                                               obuf[:, c, j * P:(j + 1) * P], ident[:, :])
                last.then_inc(o_turned, 1)
            wait(pe, y_used, t)
            for c in range(B):
                pe.wait_ge(oT_ready, 2 * t + c + 1)
                for j in range(4):
                    last = mm_(bank[2][:, c * D:(c + 1) * D], oT[:, c, j * P:(j + 1) * P], wo_sb[:, j, :],
                               start=(c == 0 and j == 0), stop=(j == 3), skip_group_check=True)
            last.then_inc(y_made, 1)

        def route(t):
            pe.wait_ge(xf_ready, t + 1)
            wait(pe, xf_moved, t)
            for c in range(B):
                for k in range(DK):
                    last = nc.tensor.transpose(bank[4][:, (c * DK + k) * P:(c * DK + k + 1) * P],
                                               yn[:, c, k * P:(k + 1) * P], ident[:, :])
            last.then_inc(xf_turned, 1)
            pe.wait_ge(xf_stat, t + 1)
            wait(pe, logits_ready, t)
            for c in range(B):
                for k in range(DK):
                    last = mm_(bank[5][:, c * E:(c + 1) * E], xfb[:, c, k, :], wr[:, k, :],
                               start=(c == 0 and k == 0), stop=(k == DK - 1), skip_group_check=True)
            last.then_inc(logits_made, 1)

        out_projection(0)

        def stage_c(t):
            if not (isinstance(t, int) and t == TQ - 1):
                out_projection(t + 1)
            route(t)

        pair_loop(pe, stage_c, TQ)

        pe.wait_ge(taken_ready, 1)
        pe.wait_ge(d_consts, 1)
        mm_(bank[6][:, 0:E], upper[:, :], taken[:, :], start=True, stop=True)
        mm_(bank[7][:, 0:E], allones[:, :], taken[:, :], start=True, stop=True).then_inc(counts_made, 1)

        def hidden(g, u):
            n = SU * g + u
            wait(pe, hid_ready, n - 1)
            for w in range(2):
                for k in range(DK):
                    last = mm_(bank[2 * (u % 2) + w][:, :], w12s[:, k, w, u * P:(u + 1) * P],
                               xfT[:, k, bass.ds(g * GR, GR)], start=(k == 0), stop=(k == DK - 1))
            last.then_inc(hid_made, 1)

        def down(g, u):
            pe.wait_ge(hid_ready, SU * g + u + 1)
            if u == 0:
                wait(pe, ysh_added, g)
            for j in range(4):
                last = mm_(bank[4 + j // 2][:, (j % 2) * D:(j % 2 + 1) * D], gsh[:, u % 2, j * P:(j + 1) * P],
                           w3s[:, u, :], start=(u == 0 and j % 2 == 0), stop=(u == SU - 1), skip_group_check=True)
            if u == SU - 1:
                last.then_inc(ysh_made, 1)

        def shared(g):
            for u in range(SU):
                hidden(g, u)
                if u:
                    down(g, u - 1)
            down(g, SU - 1)

        pe.wait_ge(ws_loaded, 48)
        pe.wait_ge(xf_moved, TQ)
        pe.wait_ge(score_ready, 1)
        pe.wait_ge(routed, 1)
        for g in range(NG // 2):
            shared(g)

        pe.wait_ge(wr_loaded, 16 * 3 * E)
        pe.wait_ge(ysh_added, NG // 2)

        def turn_slot(s, i, c):
            pe.wait_ge(slot_loaded[c % 4], 16 * (i + c // 4 + 1))
            for k in range(DK):
                last = nc.tensor.transpose(bank[c % 2][:, k * P:(k + 1) * P], xsl[:, c % 4, k * P:(k + 1) * P],
                                           ident[:, :])
            last.then_inc(slot_turned, 1)

        def slot_hidden(s, p):
            e = nc.tensor.value_load(exps[0:1, bass.ds(s, 1)], min_val=0, max_val=E - 1)
            pe.wait_ge(slotT_ready, s + 1)
            wait(pe, rg_ready, s - 1)
            for k in range(DK):
                last = mm_(bank[2 + p][:, :], xsT[:, p, k, :], w12r[:, e, k, :],
                           start=(k == 0), stop=(k == DK - 1))
            last.then_inc(rh_made, 1)

        def turn_hidden(s, p):
            pe.wait_ge(rg_ready, s + 1)
            for k in range(2):
                last = nc.tensor.transpose(bank[4 + p][:, k * P:(k + 1) * P], rg[:, p, k * P:(k + 1) * P], ident[:, :])
            last.then_inc(rg_turned, 1)

        def slot_down(s, p):
            e = nc.tensor.value_load(exps[0:1, bass.ds(s, 1)], min_val=0, max_val=E - 1)
            pe.wait_ge(rgT_ready, s + 1)
            wait(pe, yo_ready, s - 1)
            for k in range(2):
                last = mm_(bank[6 + p][:, 0:D], rgT[:, p, k * P:(k + 1) * P], w3r[:, e, k, :],
                           start=(k == 0), stop=(k == 1))
            last.then_inc(ry_made, 1)

        def slot(s, i, c):
            if inside(s):
                slot_hidden(s, c % 2)
            if inside(s + 1):
                turn_slot(s + 1, i, c + 1)
            if inside(s - 1):
                turn_hidden(s - 1, (c + 1) % 2)
            if inside(s - 2):
                slot_down(s - 2, c % 2)

        turn_slot(0, 0, 0)
        slot_loop(pe, slot)

        pe.wait_ge(yo_ready, NS)
        for g in range(NG // 2, NG):
            shared(g)

    @block.scalar
    def _(act):
        a = nc.scalar.activation
        act.wait_ge(consts_made, 1)
        act.wait_ge(zeros_made, 1)
        act.wait_ge(consts_loaded, 16 * NC_CONST)

        def deviations(first):
            act.wait_ge(var_ready, first)
            a(sd[:, :, :], mv[:, :, 1:2], ACT.Sqrt, bias=eps[:, :]).then_inc(sd_ready, 1)

        def affine(n, c, kind):
            act.wait_ge(xt_turned, n + 1)
            for k in range(DK):
                last = a(xT[:, c, k, :], bank[c][:, k * P:(k + 1) * P], ACT.Identity,
                         scale=lnw[:, kind, 0, k:k + 1], bias=lnw[:, kind, 1, k:k + 1])
            last.then_inc(xT_ready, 1)

        def squares(t, n, c, latent, sq_at):
            wait(act, ssq_ready, n)
            if latent:
                act.wait_ge(q_made, n + 1)
                a(sq[:, 0, :], bank[2 + 3 * c][:, :], ACT.Square).then_inc(sq_ready, 1)
            act.wait_ge(k_made, n + 1)
            a(sq[:, 1, :], bank[3 + 3 * c][:, :], ACT.Square).then_inc(sq_ready, 1)
            act.wait_ge(v_made, n + 1)
            a(vn[:, c * H:(c + 1) * H, t, 0:DH], bank[4 + 3 * c][:, :].rearrange("p (h d) -> p h d", d=DH),
              ACT.Copy).then_inc(v_used, 1)

        def norms(n):
            act.wait_ge(ssq_ready, n + 1)
            a(nrm[:, :], ssq[:, :], ACT.Sqrt).then_inc(nrm_ready, 1)

        deviations(1)
        deviations(2)
        for c in range(B):
            affine(c, c, 0)

        def stage_a(t):
            if isinstance(t, int) and t == TQ - 1:
                deviations(2 * TQ + 1)
                kind = 1
            else:
                deviations(2 * t + 3)
                deviations(2 * t + 4)
                kind = 0
            for c in range(B):
                squares(t, 2 * t + c, c, True, 0)
                affine(2 * t + 2 + c, c, kind)
                norms(2 * t + c)

        pair_loop(act, stage_a, TQ)
        for c in range(B):
            squares(TQ, NT + c, c, False, 0)
            norms(NT + c)

        act.wait_ge(masks_made, 1)
        act.wait_ge(k_used, NT + B)

        def scale_head(hh, p, g):
            what, first, n = TURNS[g]
            act.wait_ge(heads_turned, NTURN * hh + g + 1)
            cols = slice(first * P, (first + n) * P)
            src = bank[TURN_BANK[g]]
            if what == "k":
                a(kT1[p][:, cols], src[:, 0:n * P], ACT.Copy, scale=qks[:, 1:2]).then_inc(scaled, 1)
            else:
                a(qT1[p][:, cols], src[:, 0:n * P], ACT.Copy, scale=qks[:, 0:1])
                a(qT2[p][0:DH, cols], src[0:DH, 0:n * P], ACT.Copy, scale=qks[0:DH, 0:1]).then_inc(scaled, 1)

        def keep_neg(hh, p):
            for z in range(2):
                act.wait_ge(neg_turned, 2 * hh + z + 1)
                a(qT2[p][DH:DH + 1, z * QC:(z + 1) * QC], bank[NEG_BANK[z]][DH:DH + 1, :],
                  ACT.Copy).then_inc(neg_row, 1)

        def exponentials(hh, p, s):
            act.wait_ge(scores_made, STEPS * hh + s + 1)
            wait(act, pv_done, STEPS * hh + s - 2)
            bias = mbias[p][:, :] if s % TK == TK - 1 else zero[:, :]
            a(prob[:, s % 3, :], bank[s % 2][:, :], ACT.Exp, bias=bias).then_inc(probs_ready, 1)

        for g in range(NTURN):
            scale_head(0, 0, g)
        keep_neg(0, 0)

        def stage_b(hh, p, prepare):
            for s in range(STEPS):
                exponentials(hh, p, s)
                if prepare and s < NTURN:
                    scale_head(hh + 1, 1 - p, s)
            if prepare:
                keep_neg(hh + 1, 1 - p)

        head_loop(act, stage_b)

        act.wait_ge(c_loaded, 64)

        def copy_oT(t):
            for c in range(B):
                act.wait_ge(o_turned, 2 * t + c + 1)
                a(oT[:, c, :], bank[c][:, :], ACT.Copy).then_inc(oT_ready, 1)

        def deviations_c(k):
            act.wait_ge(cvar_ready, k)
            a(sd[:, :, :], mv[:, :, 1:2], ACT.Sqrt, bias=eps[:, :]).then_inc(csd_ready, 1)

        copy_oT(0)

        def stage_c(t):
            deviations_c(2 * t + 1)
            if not (isinstance(t, int) and t == TQ - 1):
                copy_oT(t + 1)
            deviations_c(2 * t + 2)
            act.wait_ge(xf_turned, t + 1)
            src = bank[4][:, :].rearrange("p (c k n) -> p c k n", c=B, k=DK)
            a(xfb[:, :, :, :], src, ACT.Copy).then_inc(xf_stat, 1)
            for c in range(B):
                last = a(xfT[:, :, bass.ds((2 * t + c) * P, P)], src[:, c, :, :], ACT.Copy)
            last.then_inc(xf_moved, 1)
            act.wait_ge(logits_made, t + 1)
            a(logits[:, bass.ds(2 * t, 2), :], bank[5][:, 0:2 * E].rearrange("p (c e) -> p c e", c=B),
              ACT.Copy).then_inc(logits_ready, 1)

        pair_loop(act, stage_c, TQ)

        act.drain()
        a(score[:, :, :], logits[:, :, :], ACT.Sigmoid).then_inc(score_ready, 1)

        def shared(g):
            for u in range(SU):
                n = SU * g + u
                act.wait_ge(hid_made, n + 1)
                wait(act, hid_ready, n - 1)
                a(sil[:, u % 2, :], bank[2 * (u % 2)][:, :], ACT.Silu).then_inc(sil_ready, 1)

        for g in range(NG // 2):
            shared(g)

        def copy_slotT(s, p):
            act.wait_ge(slot_turned, s + 1)
            a(xsT[:, p, :, :], bank[p][:, 0:D].rearrange("p (k n) -> p k n", k=DK), ACT.Copy).then_inc(slotT_ready, 1)

        def slot_silu(s, p):
            act.wait_ge(rh_made, s + 1)
            wait(act, rg_ready, s - 1)
            a(sil[:, p, 0:HID], bank[2 + p][:, 0:HID], ACT.Silu).then_inc(rsil_ready, 1)

        def copy_result(s, p, before):
            act.wait_ge(ry_made, s + 1)
            wait(act, yo_stored[p], 16 * before)
            a(yo[:, p, :], bank[6 + p][:, 0:D], ACT.Copy).then_inc(yo_ready, 1)

        def slot(s, i, c):
            if inside(s):
                slot_silu(s, c % 2)
            if inside(s + 1):
                copy_slotT(s + 1, (c + 1) % 2)
            if inside(s - 2):
                copy_result(s - 2, c % 2, 2 * i + (c - 2) // 2)

        copy_slotT(0, 0)
        slot_loop(act, slot)

        for g in range(NG // 2, NG):
            shared(g)

    @block.vector
    def _(dve):
        v = nc.vector

        def moments(src, made):
            for c in range(B):
                v.bn_stats(st[:, c, :], src(c))
            v.drain()
            for c in range(B):
                last = v.bn_aggr(mv[:, c, :], st[:, c, :])
            last.then_inc(made, 1)

        def normalise(dst, src, done=None):
            v.reciprocal(rs[:, :, :], sd[:, :, :])
            v.drain()
            for c in range(B):
                last = v.tensor_scalar(dst(c), src(c), mv[:, c, 0:1], rs[:, c, :], ALU.subtract, ALU.mult)
            if done is not None:
                last.then_inc(done, 1)
            v.drain()

        def norm_pair(t, kind):
            dve.wait_ge(x_loaded, 32 * (t + 1) + (32 if kind else 0))
            xin_ = lambda c: xin[:, c, :]
            moments(xin_, var_ready)
            dve.wait_ge(sd_ready, 2 * t + 1)
            if kind:
                wait(dve, xt_turned, 2 * t)
                normalise(lambda c: xn2[:, c, :], xin_, xnorm_ready)
                return
            normalise(lambda c: xn[:, c, :], xin_, x_used)
            moments(lambda c: xn[:, c, :], var_ready)
            dve.wait_ge(sd_ready, 2 * t + 2)
            wait(dve, xt_turned, 2 * t)
            normalise(lambda c: xn2[:, c, :], lambda c: xn[:, c, :], xnorm_ready)

        def l2norm(t, n, c, latent, sq_at):
            parts = ((0, q_used, on), (1, k_used, kn)) if latent else ((1, k_used, kn),)
            for j, (i, _, _) in enumerate(parts):
                dve.wait_ge(sq_ready, sq_at + j + 1)
                last = v.tensor_reduce(ssq[:, i * H:(i + 1) * H], sq[:, i, :].rearrange("p (h d) -> p h d", d=DH),
                                       AX.X, ALU.add)
            last.then_inc(ssq_ready, 1)
            dve.wait_ge(nrm_ready, n + 1)
            v.tensor_scalar(rnr[:, :], nrm[:, :], L2_EPS, None, ALU.max)
            v.drain()
            v.reciprocal(rnr[:, :], rnr[:, :])
            v.drain()
            for i, used, dst in parts:
                v.tensor_tensor(dst[:, c * H:(c + 1) * H, t, :], bank[2 + 3 * c + i][:, :].rearrange("p (h d) -> p h d", d=DH),
                                rnr[:, i * H:(i + 1) * H].unsqueeze(2).to_broadcast([P, H, DH]),
                                ALU.mult).then_inc(used, 1)
            v.drain()

        norm_pair(0, 0)

        def stage_a(t):
            norm_pair(t + 1, 1 if isinstance(t, int) and t == TQ - 1 else 0)
            for c in range(B):
                l2norm(t, 2 * t + c, c, True, 2 * (2 * t + c))

        pair_loop(dve, stage_a, TQ)
        for c in range(B):
            l2norm(TQ, NT + c, c, False, 2 * NT + c)

        dve.wait_ge(masks_made, 1)

        def split_head(hh, p, g):
            what, first, n = TURNS[g]
            cols = slice(first * P, (first + n) * P)
            src = bank[TURN_BANK[g]]
            dve.wait_ge(scaled, NTURN * hh + g + 1)
            if what == "k":
                v.scalar_tensor_tensor(kT2[p][0:DH, cols], src[0:DH, 0:n * P], qks[0:DH, 1:2], kT1[p][0:DH, cols],
                                       ALU.mult, ALU.subtract).then_inc(split, 1)
            else:
                v.scalar_tensor_tensor(qT1[p][DH:P, cols], src[DH:P, 0:n * P], qks[DH:P, 0:1], qT1[p][DH:P, cols],
                                       ALU.mult, ALU.subtract).then_inc(split, 1)

        def reduce_piece(hh, k):
            tile, c = divmod(k, len(PIECES))
            dve.wait_ge(piece_made, NP_ * hh + k + 1)
            v.tensor_reduce(mx[:, tile, c:c + 1], bank[2 + k % 2][:, 0:PIECES[c][1]], AX.X, ALU.max)\
                .then_inc(piece_used, 1)

        def negate(hh, p):
            v.tensor_scalar(mbias[p][:, :], maskf[:, bass.ds(hh, 1)], 0.0, None, ALU.add)
            v.drain()
            v.tensor_reduce(mm[:, :], mx[:, :, :], AX.X, ALU.max)
            v.drain()
            wait(dve, neg_turned, 2 * hh)
            v.tensor_scalar(zneg[:, :, DH], mm[:, :], -1.0, None, ALU.mult).then_inc(neg_ready, 1)

        def divide(hh, c):
            dve.wait_ge(pv_done, STEPS * hh + TK * (c + 1))
            sums = bank[4 + c][:, 0:4 * (DH + 1)].rearrange("p (j d) -> p j d", d=DH + 1)
            v.reciprocal(rec[:, c, :], sums[:, :, DH])
            v.drain()
            v.tensor_tensor(on[:, hh, 4 * c:4 * c + 4, :], sums[:, :, 0:DH],
                            rec[:, c, :].unsqueeze(2).to_broadcast([P, 4, DH]), ALU.mult).then_inc(o_ready, 1)

        for g in range(NTURN):
            split_head(0, 0, g)
        for k in range(NP_):
            reduce_piece(0, k)
        negate(0, 0)

        def stage_b(hh, p, prepare):
            for s in range(STEPS):
                if prepare and s < NTURN:
                    split_head(hh + 1, 1 - p, s)
                if prepare:
                    for k in piece_steps.get(s, ()):
                        reduce_piece(hh + 1, k)
                if s == TK:
                    divide(hh, 0)
            if prepare:
                negate(hh + 1, 1 - p)
            divide(hh, 1)

        head_loop(dve, stage_b)

        v.drain()
        dve.wait_ge(c_loaded, 64)

        def gather_heads(t):
            wait(dve, o_turned, 2 * t)
            v.tensor_copy(obuf[:, :, :].rearrange("p c (h d) -> p (c h) d", d=DH), on[:, :, t, :]).then_inc(ob_ready, 1)

        gather_heads(0)

        def stage_c(t):
            if not (isinstance(t, int) and t == TQ - 1):
                gather_heads(t + 1)
            dve.wait_ge(y_made, t + 1)
            y = lambda c: bank[2][:, c * D:(c + 1) * D]
            moments(y, cvar_ready)
            dve.wait_ge(csd_ready, 2 * t + 1)
            wait(dve, xf_kept, t)
            wait(dve, xf_turned, t)
            normalise(lambda c: yn[:, c, :], y, y_used)
            v.tensor_tensor(yn[:, :, :], yn[:, :, :], lno[:, 0, :].unsqueeze(1).to_broadcast([P, 2, D]), ALU.mult)
            v.drain()
            dve.wait_ge(xres_ready, t + 1)
            v.tensor_tensor(x2[:, bass.ds(2 * t, 2), :], yn[:, :, :], xres[:, :, :], ALU.add).then_inc(xres_used, 1)
            v.drain()
            x2_ = lambda c: x2[:, bass.ds(2 * t + c, 1), :].rearrange("p a d -> p (a d)")
            moments(x2_, cvar_ready)
            dve.wait_ge(csd_ready, 2 * t + 2)
            normalise(lambda c: yn[:, c, :], x2_, xf_ready)

        pair_loop(dve, stage_c, TQ)

        dve.wait_ge(score_ready, 1)
        dve.wait_ge(d_consts, 1)

        def over_tiles(ap):
            return ap.unsqueeze(1).to_broadcast([P, NT, E])

        def over_experts(ap):
            return ap.unsqueeze(2).to_broadcast([P, NT, E])

        v.tensor_tensor(sel[:, :, :], score[:, :, :], over_tiles(ebias[:, :]), ALU.add)
        v.drain()
        for k in range(TOP):
            v.tensor_reduce(best[:, :], sel[:, :, :], AX.X, ALU.max)
            v.drain()
            v.tensor_tensor(work[0][:, :, :], sel[:, :, :], over_experts(best[:, :]), ALU.is_equal)
            v.drain()
            v.tensor_tensor(work[0][:, :, :], work[0][:, :, :], over_tiles(number[:, :]), ALU.mult)
            v.drain()
            v.tensor_reduce(best[:, :], work[0][:, :, :], AX.X, ALU.min)
            v.drain()
            v.tensor_tensor(onehot[k][:, :, :], over_tiles(number[:, :]), over_experts(best[:, :]), ALU.is_equal)
            v.drain()
            if k < TOP - 1:
                v.scalar_tensor_tensor(sel[:, :, :], onehot[k][:, :, :], MASKED, sel[:, :, :], ALU.mult, ALU.add)
            v.tensor_tensor(work[0][:, :, :], onehot[k][:, :, :], score[:, :, :], ALU.mult)
            v.drain()
            v.tensor_reduce(gate[:, :, k], work[0][:, :, :], AX.X, ALU.add)
            v.drain()
        v.tensor_tensor(work[0][:, :, :], onehot[0][:, :, :], onehot[1][:, :, :], ALU.add)
        v.drain()
        v.tensor_reduce(taken[:, :], work[0][:, :, :].rearrange("p n e -> p e n"), AX.X, ALU.add).then_inc(taken_ready, 1)
        v.memset(work[1][:, 0:1, :], 0.0)
        v.tensor_copy(work[1][:, 1:NT, :], work[0][:, 0:NT - 1, :])
        v.drain()
        src, step = 1, 1
        while step < NT:
            v.tensor_copy(work[1 - src][:, 0:step, :], work[src][:, 0:step, :])
            v.tensor_tensor(work[1 - src][:, step:NT, :], work[src][:, step:NT, :], work[src][:, 0:NT - step, :], ALU.add)
            v.drain()
            src, step = 1 - src, 2 * step
        before = work[src]
        dve.wait_ge(counts_made, 1)
        v.tensor_scalar(tiles_f[:, :], bank[7][:, 0:E], float(P - 1), None, ALU.add)
        v.drain()
        v.tensor_copy(tiles_i[:, :], tiles_f[:, :])
        v.drain()
        v.tensor_scalar(tiles_i[:, :], tiles_i[:, :], P.bit_length() - 1, None, ALU.logical_shift_right)
        v.drain()
        v.tensor_copy(tiles_f[:, :], tiles_i[:, :])
        v.drain()
        v.tensor_copy(ends[0][:, :], tiles_f[:, :])
        v.drain()
        src, step = 0, 1
        while step < E:
            v.tensor_copy(ends[1 - src][:, 0:step], ends[src][:, 0:step])
            v.tensor_tensor(ends[1 - src][:, step:E], ends[src][:, step:E], ends[src][:, 0:E - step], ALU.add)
            v.drain()
            src, step = 1 - src, 2 * step
        end = ends[src]
        v.tensor_tensor(offs[:, :], end[:, :], tiles_f[:, :], ALU.subtract)
        v.drain()
        v.tensor_scalar(offs[:, :], offs[:, :], float(P), None, ALU.mult)
        v.drain()
        v.tensor_tensor(offs[:, :], offs[:, :], bank[6][:, 0:E], ALU.add)
        v.drain()
        v.tensor_tensor(before[:, :, :], before[:, :, :], over_tiles(offs[:, :]), ALU.add)
        v.drain()
        for k in range(TOP):
            v.tensor_tensor(sel[:, :, :], onehot[k][:, :, :], before[:, :, :], ALU.mult)
            v.drain()
            v.tensor_reduce(posf[:, :], sel[:, :, :], AX.X, ALU.add)
            v.drain()
            v.tensor_copy(posi[:, :, k], posf[:, :])
            v.drain()
        v.tensor_tensor(passed[:, :, :], end[0:1, :].unsqueeze(1).to_broadcast([1, NS + 1, E]),
                        slot_f[:, :].unsqueeze(2).to_broadcast([1, NS + 1, E]), ALU.is_le)
        v.drain()
        v.tensor_reduce(passed_sum[:, :], passed[:, :, :], AX.X, ALU.add)
        v.drain()
        v.tensor_scalar(passed_sum[:, :], passed_sum[:, :], float(E - 1), None, ALU.min)
        v.drain()
        v.tensor_copy(exps[0:1, :], passed_sum[:, :])
        v.drain().then_inc(routed, 1)

        def product(g, u):
            n = SU * g + u
            dve.wait_ge(sil_ready, n + 1)
            v.tensor_tensor(gsh[:, u % 2, :], sil[:, u % 2, :], bank[2 * (u % 2) + 1][:, :], ALU.mult).then_inc(hid_ready, 1)

        def add_shared(g):
            dve.wait_ge(ysh_made, g + 1)
            for j in range(2):
                rows = x2[:, bass.ds(4 * g + 2 * j, 2), :]
                last = v.tensor_tensor(rows, bank[4 + j][:, :].rearrange("p (c d) -> p c d", c=2), rows, ALU.add)
            last.then_inc(ysh_added, 1)
            v.drain()

        for g in range(NG // 2):
            for u in range(SU):
                product(g, u)
            add_shared(g)

        def slot_product(s, p):
            dve.wait_ge(rsil_ready, s + 1)
            wait(dve, rg_turned, s - 1)
            v.tensor_tensor(rg[:, p, :], sil[:, p, 0:HID], bank[2 + p][:, HID:], ALU.mult).then_inc(rg_ready, 1)

        def copy_hidT(s, p):
            dve.wait_ge(rg_turned, s + 1)
            wait(dve, ry_made, s - 1)
            v.tensor_copy(rgT[:, p, :], bank[4 + p][:, 0:HID]).then_inc(rgT_ready, 1)

        def slot(s, i, c):
            if inside(s - 1):
                copy_hidT(s - 1, (c + 1) % 2)
            if inside(s):
                slot_product(s, c % 2)

        slot_loop(dve, slot)

        def combine(n):
            dve.wait_ge(gathered[n % 4], 32 * (n // 4 + 1))
            for k in range(TOP):
                last = v.scalar_tensor_tensor(x2[:, n, :], gat[n % 4][:, k, :], gate[:, n, k:k + 1], x2[:, n, :],
                                              ALU.mult, ALU.add)
                if k < TOP - 1:
                    v.drain()
            last.then_inc(combined, 1)

        done = 0
        for g in range(NG // 2, NG):
            for u in range(SU):
                product(g, u)
                if done < 4 * g and u % 2 == 1:
                    combine(done)
                    done += 1
            add_shared(g)
        while done < NT:
            combine(done)
            done += 1

    es.close()


_INS = ["x", "ctx_1024", "mask_BxS2_bk0", "L0_xattn_ln_x_w", "L0_xattn_ln_x_b", "L0_xattn_ln_l_w",
        "L0_xattn_ln_l_b", "L0_xattn_Wq", "L0_xattn_Wkv", "L0_xattn_q_scale", "L0_xattn_k_scale",
        "L0_xattn_Wo", "L0_xattn_ln_o_w", "L0_xattn_ln_o_b", "L0_ffn_router_w", "L0_ffn_expert_bias",
        "L0_ffn_shared_w1", "L0_ffn_shared_w2", "L0_ffn_shared_w3", "L0_ffn_routed_w1",
        "L0_ffn_routed_w2", "L0_ffn_routed_w3"]


def kernel(**inputs):
    import numpy as np
    import concourse.bacc as bacc
    from concourse.bass_utils import run_bass_kernel_spmd

    nc = bacc.Bacc("TRN2", target_bir_lowering=False, num_devices=1)
    arrays, args = {}, []
    for name in _INS:
        a = np.ascontiguousarray(inputs[name])
        if a.dtype == np.bool_:
            a = a.astype(np.int32)
        arrays[f"in_{name}"] = a
        args.append(nc.dram_tensor(f"in_{name}", a.shape, mybir.dt.from_np(a.dtype), kind="ExternalInput").ap())
    out = nc.dram_tensor("out", (B, S, D), F32, kind="ExternalOutput").ap()
    build(nc, *args, out)
    r = run_bass_kernel_spmd(nc, [arrays], core_ids=[0])
    return r.results[0]["out"]
```

```python
from contextlib import ExitStack

import concourse.bass as bass
from concourse import mybir

F32 = mybir.dt.float32
F32R = mybir.dt.float32r
I32 = mybir.dt.int32
ACT = mybir.ActivationFunctionType
ALU = mybir.AluOpType
AX = mybir.AxisListType

B, S, D = 2, 1024, 256
M = 64
H, DH = 8, 64
INNER = H * DH
P = 128
DK = D // P
TQ = S // P
TK = TQ + 1
NT = B * TQ
BH = B * H
QC = 512
CH = S // QC
STEPS = CH * TK
SCALE = 8.0
LN_EPS, L2_EPS = 1e-5, 1e-12
MASKED = -1e30
E, HID = 16, 256
SH = 1024
SU = SH // P
GR = 512
NG = NT * P // GR
TOP = 2
NS = (TOP * NT * P + E * (P - 1)) // P
FAR = 99.0
KEYS = S + M
PIECES = [(0, 384), (384, 384), (768, KEYS - 768)]
NP_ = len(PIECES) * TQ


def wait(eng, sem, value):
    if isinstance(value, int) and value <= 0:
        return
    eng.wait_ge(sem, value)


def build(nc, x, ctx, mask, ln_x_w, ln_x_b, ln_l_w, ln_l_b, wq, wkv, q_scale, k_scale, wo,
          ln_o_w, ln_o_b, router_w, expert_bias, sw1, sw2, sw3, rw1, rw2, rw3, out, dbg=None):
    es = ExitStack()

    def sb(name, shape, dt=F32, stack=es):
        return stack.enter_context(nc.sbuf_tensor(name, shape, dt))

    def sem(name):
        return es.enter_context(nc.semaphore(name))

    xs_dram = nc.dram_tensor("slot_rows", (NS * P, D), F32, kind="Internal").ap()
    ys_dram = nc.dram_tensor("slot_results", (NS * P, D), F32, kind="Internal").ap()

    ident = sb("ident", [P, P])
    eps = sb("eps", [P, 1])
    half = sb("half", [P, 2, 1])
    zero = sb("zero", [P, 1])
    zrow = sb("zrow", [P, D])
    lnw = sb("lnw", [P, 2, 2, DK])
    qks = sb("qks", [P, 2])
    maskf = sb("maskf", [P, BH])
    mask_i = sb("mask_i", [M, B], I32)
    maskrow_i = sb("maskrow_i", [1, B, M], I32)
    wr = sb("wr", [P, DK, E])
    ebias = sb("ebias", [P, E])
    exps = sb("exps", [P, NS + 1], I32)
    posi = sb("posi", [P, NT, TOP], I32)
    gate = sb("gate", [P, NT, TOP])
    logits = sb("logits", [P, NT, E])
    st = sb("st", [P, 2, 6])
    mv = sb("mv", [P, 2, 2])
    sd = sb("sd", [P, 2, 1])
    rs = sb("rs", [P, 2, 1])

    first = ExitStack()
    wqkv = sb("wqkv", [P, DK, 3 * INNER], stack=first)
    xin = sb("xin", [P, 2, D], stack=first)
    xn = sb("xn", [P, 2, D], stack=first)
    xn2 = sb("xn2", [P, 2, D], stack=first)
    xT = sb("xT", [P, 2, DK, P], stack=first)
    sq = sb("sq", [P, 2, INNER], stack=first)
    ssq = sb("ssq", [P, 2 * H], stack=first)
    nrm = sb("nrm", [P, 2 * H], stack=first)
    rnr = sb("rnr", [P, 2 * H], stack=first)
    first_end = nc.sbuf_bytes_remaining
    first.close()
    moe = ExitStack()
    xsl = sb("xsl", [P, 4, D], stack=moe)
    xsT = sb("xsT", [P, 2, DK, P], stack=moe)
    rg = sb("rg", [P, 2, HID], stack=moe)
    rgT = sb("rgT", [P, 2, HID], stack=moe)
    yo = sb("yo", [P, 2, D], stack=moe)
    gat = [sb(f"slot_result{i}", [P, TOP, D], stack=moe) for i in range(4)]
    moe.close()
    cst = ExitStack()
    wo_sb = sb("wo_sb", [P, INNER // P, D], stack=cst)
    lno = sb("lno", [P, 2, D], stack=cst)
    xres = sb("xres", [P, 2, 2, D], stack=cst)
    oT = sb("oT", [P, 2, 2, INNER], stack=cst)
    yn = sb("yn", [P, 2, D], stack=cst)
    cst.enter_context(nc.sbuf_tensor("rest_of_first", [P, (nc.sbuf_bytes_remaining - first_end) // 4], F32))

    att = ExitStack()
    on = sb("on", [P, TQ, BH, DH], stack=att)
    kn = sb("kn", [P, BH, TK, DH], stack=att)
    vn = sb("vn", [P, BH, TK, DH + 1], stack=att)
    dup = sb("dup", [P, TQ + TK, 2, DH], stack=att)
    qT1 = [sb(f"q_hi_lo{i}", [P, S], F32R, att) for i in range(2)]
    qT2 = [sb(f"q_hi_max{i}", [P, S], F32R, att) for i in range(2)]
    kT1 = [sb(f"k_hi_hi{i}", [P, TK * P], F32R, att) for i in range(2)]
    kT2 = [sb(f"k_lo_one{i}", [P, TK * P], F32R, att) for i in range(2)]
    prob = sb("prob", [P, 3, QC], stack=att)
    mx = sb("mx", [P, TQ, len(PIECES)], stack=att)
    mbias = [sb(f"mbias{i}", [P, 1], stack=att) for i in range(2)]
    mm = sb("mm", [P, TQ], stack=att)
    zneg = sb("zneg", [P, TQ, DH + 1], stack=att)
    rec = sb("rec", [P, 2, QC // P], stack=att)
    maskrow = sb("maskrow", [P, BH, M], stack=att)
    firstrow = sb("firstrow", [P, P], stack=att)
    att.close()

    ffn = ExitStack()
    w3r = sb("w3r", [P, E, HID // P, D], stack=ffn)
    x2 = sb("x2", [P, NT, D], stack=ffn)
    xf = sb("xf", [P, NT, D], stack=ffn)
    xfT = sb("xfT", [P, DK, NT * P], stack=ffn)
    w12r = sb("w12r", [P, E, DK, 2 * HID], stack=ffn)
    w12s = sb("w12s", [P, DK, 2, SH], stack=ffn)
    w3s = sb("w3s", [P, SU, D], stack=ffn)


    sil = sb("sil", [P, 2, GR], stack=ffn)
    gsh = sb("gsh", [P, 2, GR], stack=ffn)
    ffn.close()
    rt = ExitStack()
    rt.enter_context(nc.sbuf_tensor("below_routing", [P, (B * H * TQ * DH) + 3 * NT * D], F32))
    below_bytes = nc.sbuf_bytes_remaining
    onehot = [sb(f"onehot{k}", [P, NT, E], stack=rt) for k in range(TOP)]
    score = sb("score", [P, NT, E], stack=rt)
    sel = sb("sel", [P, NT, E], stack=rt)
    work = [sb(f"work{k}", [P, NT, E], stack=rt) for k in range(2)]
    best = sb("best", [P, NT], stack=rt)
    number = sb("number", [P, E], stack=rt)
    number_i = sb("number_i", [P, E], I32, rt)
    slot_i = sb("slot_i", [1, NS + 1], I32, rt)
    slot_f = sb("slot_f", [1, NS + 1], stack=rt)
    passed = sb("passed", [1, NS + 1, E], stack=rt)
    passed_sum = sb("passed_sum", [1, NS + 1], stack=rt)
    upper = sb("upper", [P, P], stack=rt)
    allones = sb("allones", [P, P], stack=rt)
    taken = sb("taken", [P, E], stack=rt)
    tiles_i = sb("tiles_i", [P, E], I32, rt)
    tiles_f = sb("tiles_f", [P, E], stack=rt)
    ends = [sb(f"ends{k}", [P, E], stack=rt) for k in range(2)]
    offs = sb("offs", [P, E], stack=rt)
    posf = sb("posf", [P, NT], stack=rt)
    rt_bytes = below_bytes - nc.sbuf_bytes_remaining
    OVER_D = -(-rt_bytes // (4 * DK * 2 * HID))
    rt.close()
    cst.close()

    bank = [es.enter_context(nc.psum_tensor(f"bank{i}", [P, 512], F32)) for i in range(8)]

    eps_made = sem("eps_made")
    consts_loaded, consts_made, masks_made = sem("consts_loaded"), sem("consts_made"), sem("masks_made")
    zeros_made, xs_zeroed = sem("zeros_made"), sem("xs_zeroed")
    x_loaded, x_used, var_ready, sd_ready = sem("x_loaded"), sem("x_used"), sem("var_ready"), sem("sd_ready")
    xnorm_ready, xt_turned, xT_ready = sem("xnorm_ready"), sem("xt_turned"), sem("xT_ready")
    q_made, k_made, v_made = sem("q_made"), sem("k_made"), sem("v_made")
    sq_ready, ssq_ready, nrm_ready = sem("sq_ready"), sem("ssq_ready"), sem("nrm_ready")
    q_used, k_used, v_used = sem("q_used"), sem("k_used"), sem("v_used")
    dup_ready, heads_turned, scaled, split = sem("dup_ready"), sem("heads_turned"), sem("scaled"), sem("split")
    piece_made, piece_used = sem("piece_made"), sem("piece_used")
    neg_ready, neg_turned, neg_row = sem("neg_ready"), sem("neg_turned"), sem("neg_row")
    scores_made, probs_ready, pv_done = sem("scores_made"), sem("probs_ready"), sem("pv_done")
    o_ready = sem("o_ready")
    c_loaded, xres_ready, xres_used = sem("c_loaded"), sem("xres_ready"), sem("xres_used")
    xres_loaded = [sem(f"xres_loaded{i}") for i in range(2)]
    o_turned, oT_ready = sem("o_turned"), sem("oT_ready")
    y_made, y_used, cvar_ready, crs_ready = sem("y_made"), sem("y_used"), sem("cvar_ready"), sem("crs_ready")
    xf_ready, xf_turned, xf_moved = sem("xf_ready"), sem("xf_turned"), sem("xf_moved")
    logits_made, logits_ready = sem("logits_made"), sem("logits_ready")
    d_consts, score_ready, taken_ready, counts_made, routed = (sem("d_consts"), sem("score_ready"),
                                                              sem("taken_ready"), sem("counts_made"), sem("routed"))
    scattered = sem("scattered")
    ws_loaded, wr_loaded = sem("shared_weights_loaded"), sem("routed_weights_loaded")
    hid_made, sil_ready, hid_ready, ysh_made, ysh_added = (sem("hid_made"), sem("sil_ready"), sem("hid_ready"),
                                                         sem("ysh_made"), sem("ysh_added"))
    slot_loaded = [sem(f"slot_loaded{i}") for i in range(4)]
    slot_turned, slotT_ready, rh_made, rsil_ready, rg_ready = (sem("slot_turned"), sem("slotT_ready"),
                                                             sem("rh_made"), sem("rsil_ready"), sem("rg_ready"))
    rg_turned, rgT_ready, ry_made, yo_ready = sem("rg_turned"), sem("rgT_ready"), sem("ry_made"), sem("yo_ready")
    yo_stored = [sem(f"yo_stored{i}") for i in range(2)]
    gathered = [sem(f"gathered{i}") for i in range(4)]
    combined, out_stored = sem("combined"), sem("out_stored")

    NC_CONST = 20

    def pair_loop(eng, body, n):
        body(0)
        with eng.Fori(1, n - 1) as t:
            body(t)
        body(n - 1)

    def head_loop(eng, body):
        body(0, 0, True)
        body(1, 1, True)
        with eng.Fori(1, BH // 2 - 1) as i:
            body(2 * i, 0, True)
            body(2 * i + 1, 1, True)
        body(BH - 2, 0, True)
        body(BH - 1, 1, False)

    def inside(s):
        return not isinstance(s, int) or 0 <= s < NS

    def slot_loop(eng, body):
        for c in range(4):
            body(c, 0, c)
        with eng.Fori(1, NS // 4) as i:
            for c in range(4):
                body(4 * i + c, i, c)
        for s in range(NS // 4 * 4, NS + 2):
            body(s, s // 4, s % 4)

    piece_steps, at = {}, 0
    for s in range(5, 16):
        n = 3 if s >= 14 else 2
        piece_steps[s] = range(at, at + n)
        at += n
    assert at == NP_
    TURNS = [("k", 0, 4), ("k", 4, 4), ("k", 8, 1), ("q", 0, 4), ("q", 4, 4)]
    NTURN = len(TURNS)
    TURN_BANK = [6, 7, 6, 7, 6]
    NEG_BANK = [7, 6]

    GB = NG - 1
    FIRST = 2

    COUNT_AT = 17

    def beside(n):
        t = FIRST + n // 2
        return t if n >= 0 and n % 2 == 0 and t < TQ else None

    def cbanks(t):
        i = 4 if t == 0 else 6
        return bank[i], bank[i + 1]

    block = es.enter_context(nc.Block())

    @block.sync
    def _(sp):
        c = consts_loaded
        for kind, vecs in enumerate(((ln_l_w, ln_l_b), (ln_x_w, ln_x_b))):
            for i, vec in enumerate(vecs):
                for k in range(DK):
                    sp.dma_start(lnw[:, kind, i, k:k + 1],
                                 vec[k * P:(k + 1) * P].rearrange("(p a) -> p a", a=1)).then_inc(c, 16)

        def load_x(t, kind):
            wait(sp, x_used, t)
            for b in range(B):
                if kind == "latent":
                    sp.dma_start(xin[:, b, :], x[b, bass.ds(t * P, P), :]).then_inc(x_loaded, 16)
                else:
                    for r in range(P // M):
                        sp.dma_start(xin[r * M:(r + 1) * M, b, :], ctx[b, :, :]).then_inc(x_loaded, 16)

        load_x(0, "latent")
        for k in range(DK):
            sp.dma_start(wqkv[:, k, 0:INNER], wq[k * P:(k + 1) * P, :]).then_inc(c, 16)
            sp.dma_start(wqkv[:, k, INNER:], wkv[k * P:(k + 1) * P, :]).then_inc(c, 16)
        for r in range(2):
            sp.dma_start(qks[r * DH:(r + 1) * DH, 0:1], q_scale.rearrange("(p a) -> p a", a=1)).then_inc(c, 16)
            sp.dma_start(qks[r * DH:(r + 1) * DH, 1:2], k_scale.rearrange("(p a) -> p a", a=1)).then_inc(c, 16)
        for b in range(B):
            sp.dma_start(mask_i[:, b:b + 1], mask[b, :].rearrange("(m a) -> m a", a=1)).then_inc(c, 16)
        sp.dma_start(maskrow_i[:, :, :], mask.rearrange("(a b) m -> a b m", a=1)).then_inc(c, 16)
        sp.dma_start(wr[:, :, :], router_w.rearrange("(k p) e -> p k e", p=P)).then_inc(c, 16)
        with sp.Fori(1, TQ) as t:
            load_x(t, "latent")
        load_x(TQ, "context")

        sp.wait_ge(zeros_made, 1)
        for s in range(NS):
            sp.dma_start(xs_dram[s * P:(s + 1) * P, :], zrow[:, :]).then_inc(xs_zeroed, 16)

        sp.wait_ge(q_used, NT)
        sp.wait_ge(k_used, NT + B)
        sp.wait_ge(v_used, NT + B)
        sp.dma_start(wo_sb[:, :, :], wo.rearrange("(k p) d -> p k d", p=P)).then_inc(c_loaded, 16)
        sp.dma_start(lno[:, 0, :], ln_o_w.rearrange("(a d) -> a d", a=1).to_broadcast([P, D])).then_inc(c_loaded, 16)
        sp.dma_start(lno[:, 1, :], ln_o_b.rearrange("(a d) -> a d", a=1).to_broadcast([P, D])).then_inc(c_loaded, 16)
        sp.dma_start(ebias[:, :], expert_bias.rearrange("(a d) -> a d", a=1).to_broadcast([P, E])).then_inc(c_loaded, 16)

        def load_res(t):
            wait(sp, xres_used, t - 1)
            for b in range(B):
                sp.dma_start(xres[:, t % 2, b, :], x[b, bass.ds(t * P, P), :]).then_inc(xres_loaded[t % 2], 16)

        load_res(0)
        load_res(1)
        sp.wait_ge(o_ready, CH * BH)
        sp.wait_ge(scaled, NTURN * BH)
        for w, src in enumerate((sw1, sw2)):
            sp.dma_start(w12s[:, :, w, :], src[0].rearrange("(k p) h -> p k h", p=P)).then_inc(ws_loaded, 16)
        sp.dma_start(w3s[:, :, :], sw3[0].rearrange("(u p) d -> p u d", p=P)).then_inc(ws_loaded, 16)
        for t in range(2, TQ):
            load_res(t)

        def load_w12(e):
            sp.dma_start(w12r[:, e, :, 0:HID], rw1[e].rearrange("(k p) h -> p k h", p=P)).then_inc(wr_loaded, 16)
            sp.dma_start(w12r[:, e, :, HID:], rw2[e].rearrange("(k p) h -> p k h", p=P)).then_inc(wr_loaded, 16)

        with sp.Fori(OVER_D, E) as e:
            load_w12(e)
        sp.wait_ge(o_turned, NT)
        with sp.Fori(0, E) as e:
            sp.dma_start(w3r[:, e, :, :], rw3[e].rearrange("(k p) d -> p k d", p=P)).then_inc(wr_loaded, 16)
        sp.wait_ge(routed, 1)
        for e in range(OVER_D):
            load_w12(e)

        sp.wait_ge(scattered, 16 * NT * TOP)

        def slot(s, i, c):
            if inside(s + 3):
                wait(sp, slot_turned, s)
                sp.dma_start(xsl[:, (c + 3) % 4, :], xs_dram[bass.ds((s + 3) * P, P), :])\
                    .then_inc(slot_loaded[(c + 3) % 4], 16)
            if inside(s - 2):
                sp.wait_ge(yo_ready, s - 1)
                sp.dma_start(ys_dram[bass.ds((s - 2) * P, P), :], yo[:, c % 2, :]).then_inc(yo_stored[c % 2], 16)

        for s in range(3):
            sp.dma_start(xsl[:, s, :], xs_dram[s * P:(s + 1) * P, :]).then_inc(slot_loaded[s], 16)
        slot_loop(sp, slot)

        for n in range(NT):
            sp.wait_ge(combined, n + 1)
            sp.dma_start(out[n % B, (n // B) * P:(n // B + 1) * P, :], x2[:, n, :]).then_inc(out_stored, 16)
        sp.wait_ge(out_stored, 16 * NT)

    @block.gpsimd
    def _(pool):
        g = nc.gpsimd
        g.memset(half[:, :, :], -0.5)
        g.memset(eps[:, :], LN_EPS).then_inc(eps_made, 1)
        g.memset(ident[:, :], 0.0)
        g.memset(firstrow[:, :], 0.0)
        g.memset(maskrow[:, :, :], 0.0)
        g.memset(maskf[:, :], MASKED)
        g.memset(zero[:, :], 0.0)
        g.memset(zrow[:, :], 0.0)
        g.memset(zneg[:, :, :], 0.0)
        g.memset(vn[:, :, :, DH:DH + 1], 1.0)
        g.drain()
        for i in range(2):
            g.memset(qT2[i][DH:P, :].bitcast(F32), 0.0)
            g.memset(kT2[i][DH:P, :].bitcast(F32), 0.0)
        g.drain()
        g.affine_select(out=ident[:, :], in_=ident[:, :], compare_op=ALU.not_equal, fill=1.0,
                        base=0, pattern=[[-1, P]], channel_multiplier=1)
        g.drain()
        g.memset(firstrow[0:1, :], 1.0)
        g.drain()
        for i in range(2):
            last = g.memset(kT2[i][DH:DH + 1, :].bitcast(F32), 1.0)
        last.then_inc(consts_made, 1)
        g.drain().then_inc(zeros_made, 1)
        pool.wait_ge(consts_loaded, 16 * NC_CONST)
        for b in range(B):
            for h in range(H):
                g.tensor_scalar(maskf[0:M, b * H + h:b * H + h + 1], mask_i[:, b:b + 1], -1.0, -MASKED,
                                ALU.add, ALU.mult)
                g.tensor_scalar(maskrow[0:1, b * H + h, :], maskrow_i[:, b, :], -1.0, -MASKED,
                                ALU.add, ALU.mult)
        g.tensor_scalar(qks[:, 0:1], qks[:, 0:1], SCALE, None, ALU.mult)
        g.drain().then_inc(masks_made, 1)

        pool.wait_ge(q_used, NT)
        pool.wait_ge(k_used, NT + B)

        def duplicate(hh):
            wait(pool, heads_turned, NTURN * hh)
            kin = kn[:, hh, :, :].unsqueeze(2).to_broadcast([P, TK, 2, DH])
            qin = on[:, :, hh, :].unsqueeze(2).to_broadcast([P, TQ, 2, DH])
            g.tensor_copy(dup[:, TQ:, :, :], kin)
            g.tensor_copy(dup[:, 0:TQ, :, :], qin).then_inc(dup_ready, 1)

        duplicate(0)
        with pool.Fori(1, BH) as hh:
            duplicate(hh)

        pool.wait_ge(o_ready, CH * BH)
        g.memset(upper[:, :], 1.0)
        g.memset(allones[:, :], 1.0)
        g.iota(number_i[:, :], pattern=[[1, E]], base=-int(FAR), channel_multiplier=0)
        g.iota(slot_i[:, :], pattern=[[1, NS + 1]], base=0, channel_multiplier=0)
        g.drain()
        g.tensor_copy(number[:, :], number_i[:, :])
        g.tensor_copy(slot_f[:, :], slot_i[:, :])
        g.affine_select(out=upper[:, :], in_=upper[:, :], compare_op=ALU.is_gt, fill=0.0,
                        base=0, pattern=[[1, P]], channel_multiplier=-1)
        g.drain().then_inc(d_consts, 1)

        pool.wait_ge(c_loaded, 64)
        def add_bias(t):
            pool.wait_ge(xres_loaded[t % 2], 32 * (t // 2 + 1))
            g.tensor_tensor(xres[:, t % 2, :, :], xres[:, t % 2, :, :], lno[:, 1, :].unsqueeze(1).to_broadcast([P, 2, D]),
                            ALU.add).then_inc(xres_ready, 1)

        add_bias(0)
        add_bias(1)
        for t in range(TQ):
            for k in range(2):
                pool.wait_ge(cvar_ready, 2 * t + k + 1)
                g.tensor_scalar(sd[:, :, :], mv[:, :, 1:2], LN_EPS, None, ALU.add)
                g.drain()
                g.tensor_tensor(rs[:, :, :], sd[:, :, :], half[:, :, :], ALU.pow).then_inc(crs_ready, 1)
            if t + 2 < TQ:
                add_bias(t + 2)

        pool.wait_ge(routed, 1)
        pool.wait_ge(xs_zeroed, 16 * NS)
        for n in range(NT):
            for k in range(TOP):
                g.indirect_dma_start(out=xs_dram, out_offset=bass.IndirectOffsetOnAxis(ap=posi[:, n, k:k + 1], axis=0),
                                     in_=xf[:, n, :], in_offset=None).then_inc(scattered, 16)

        for p in range(2):
            pool.wait_ge(yo_stored[p], 16 * ((NS + 1 - p) // 2))
        for n in range(NT):
            wait(pool, combined, n - 3)
            for k in range(TOP):
                g.indirect_dma_start(out=gat[n % 4][:, k, :], out_offset=None, in_=ys_dram,
                                     in_offset=bass.IndirectOffsetOnAxis(ap=posi[:, n, k:k + 1], axis=0)
                                     ).then_inc(gathered[n % 4], 16)

    @block.tensor
    def _(pe):
        mm_ = nc.tensor.matmul
        pe.wait_ge(consts_made, 1)

        def turn_x(t):
            pe.wait_ge(xnorm_ready, t + 1)
            for c in range(B):
                for k in range(DK):
                    last = nc.tensor.transpose(bank[c][:, k * P:(k + 1) * P], xn2[:, c, k * P:(k + 1) * P], ident[:, :])
                last.then_inc(xt_turned, 1)

        def project(n, c, j):
            made, used = ((q_made, q_used), (k_made, k_used), (v_made, v_used))[j]
            pe.wait_ge(xT_ready, n + 1)
            wait(pe, used, n - 1)
            for k in range(DK):
                last = mm_(bank[2 + 3 * c + j][:, :], xT[:, c, k, :], wqkv[:, k, j * INNER:(j + 1) * INNER],
                           start=(k == 0), stop=(k == DK - 1))
            last.then_inc(made, 1)

        turn_x(0)

        def stage_a(t):
            for j in range(3):
                project(2 * t, 0, j)
            for j in range(2):
                project(2 * t + 1, 1, j)
            turn_x(t + 1)
            project(2 * t + 1, 1, 2)

        pe.wait_ge(consts_loaded, 16 * NC_CONST)
        pair_loop(pe, stage_a, TQ)
        for c in range(B):
            for j in (1, 2):
                project(NT + c, c, j)

        pe.wait_ge(q_used, NT)
        pe.wait_ge(k_used, NT + B)
        pe.wait_ge(v_used, NT + B)
        pe.wait_ge(masks_made, 1)

        def turn_head(hh, g):
            what, first, n = TURNS[g]
            if g == 0:
                pe.wait_ge(dup_ready, hh + 1)
                wait(pe, neg_row, 2 * hh)
            elif g == 1:
                wait(pe, neg_row, 2 * hh - 1)
            else:
                pe.wait_ge(split, NTURN * hh + g - 1)
            first += TQ if what == "k" else 0
            for j in range(n):
                last = nc.tensor.transpose(bank[TURN_BANK[g]][:, j * P:(j + 1) * P],
                                           dup[:, first + j, :, :].rearrange("p a d -> p (a d)"), ident[:, :])
            last.then_inc(heads_turned, 1)

        def piece(hh, p, k):
            tile, c = divmod(k, len(PIECES))
            first, n = PIECES[c]
            if k == 0:
                pe.wait_ge(split, NTURN * hh + 4)
            if tile == TQ // 2 and c == 0:
                pe.wait_ge(split, NTURN * hh + 5)
            wait(pe, piece_used, NP_ * hh + k - 1)
            dst = bank[2 + k % 2]
            last = mm_(dst[:, 0:n], qT1[p][:, tile * P:(tile + 1) * P], kT1[p][:, first:first + n],
                       start=True, stop=(c < 2))
            if c == 2:
                last = mm_(dst[:, n - M:n], firstrow[:, :], maskrow[:, hh, :], start=False, stop=True)
            last.then_inc(piece_made, 1)

        def turn_neg(hh, p):
            pe.wait_ge(neg_ready, hh + 1)
            for z in range(2):
                pe.wait_ge(split, NTURN * hh + (4 if z == 0 else 5))
                for j in range(4):
                    last = nc.tensor.transpose(bank[NEG_BANK[z]][0:DH + 1, j * P:(j + 1) * P],
                                               zneg[:, 4 * z + j, :], ident[:, :])
                last.then_inc(neg_turned, 1)

        def score_tile(hh, p, s):
            c, kt = divmod(s, TK)
            if s == 0:
                pe.wait_ge(neg_row, 2 * hh + 1)
            if s == TK:
                pe.wait_ge(neg_row, 2 * hh + 2)
            if s >= 2:
                pe.wait_ge(probs_ready, STEPS * hh + s - 1)
            mm_(bank[s % 2][:, :], kT1[p][:, kt * P:(kt + 1) * P], qT1[p][:, c * QC:(c + 1) * QC],
                start=True, stop=False)
            mm_(bank[s % 2][:, :], kT2[p][:, kt * P:(kt + 1) * P], qT2[p][:, c * QC:(c + 1) * QC],
                start=False, stop=True).then_inc(scores_made, 1)

        def weigh(hh, s):
            c, kt = divmod(s, TK)
            pe.wait_ge(probs_ready, STEPS * hh + s + 1)
            if kt == 0:
                wait(pe, o_ready, CH * hh + c - 1)
            for j in range(QC // P):
                last = mm_(bank[4 + c][:, j * (DH + 1):(j + 1) * (DH + 1)], prob[:, s % 3, j * P:(j + 1) * P],
                           vn[:, hh, kt, :], start=(kt == 0 and j == 0), stop=(kt == TK - 1),
                           skip_group_check=True)
            last.then_inc(pv_done, 1)

        for g in range(NTURN):
            turn_head(0, g)
        for k in range(NP_):
            piece(0, 0, k)
        turn_neg(0, 0)

        def stage_b(hh, p, prepare):
            for s in range(STEPS):
                score_tile(hh, p, s)
                if prepare and s < NTURN:
                    turn_head(hh + 1, s)
                if prepare:
                    for k in piece_steps.get(s, ()):
                        piece(hh + 1, 1 - p, k)
                if s:
                    weigh(hh, s - 1)
            if prepare:
                turn_neg(hh + 1, 1 - p)
            weigh(hh, STEPS - 1)

        head_loop(pe, stage_b)

        pe.wait_ge(o_ready, CH * BH)
        pe.wait_ge(c_loaded, 64)

        def turn_o(t):
            for c, free in ((1, xf_moved), (0, logits_ready)):
                if t >= FIRST:
                    wait(pe, free, t)
                for j in range(4):
                    src = on[:, t, c * H + 2 * j:c * H + 2 * j + 2, :].rearrange("p a d -> p (a d)")
                    last = nc.tensor.transpose(cbanks(t)[c][:, j * P:(j + 1) * P], src, ident[:, :])
                last.then_inc(o_turned, 1)

        def project_o(t):
            pe.wait_ge(oT_ready, 2 * t + 2)
            for c in range(B):
                for j in range(4):
                    last = mm_(cbanks(t)[0][:, c * D:(c + 1) * D], oT[:, t % 2, c, j * P:(j + 1) * P], wo_sb[:, j, :],
                               start=(c == 0 and j == 0), stop=(j == 3), skip_group_check=True)
            last.then_inc(y_made, 1)

        def turn_xf(t):
            pe.wait_ge(xf_ready, t + 1)
            for c in range(B):
                for k in range(DK):
                    last = nc.tensor.transpose(cbanks(t)[1][:, (c * DK + k) * P:(c * DK + k + 1) * P],
                                               xf[:, 2 * t + c, k * P:(k + 1) * P], ident[:, :])
            last.then_inc(xf_turned, 1)

        def route(t):
            pe.wait_ge(xf_moved, t + 1)
            pe.wait_ge(y_used, t + 1)
            for c in range(B):
                n = 2 * t + c
                for k in range(DK):
                    last = mm_(cbanks(t)[0][:, c * E:(c + 1) * E], xfT[:, k, n * P:(n + 1) * P], wr[:, k, :],
                               start=(c == 0 and k == 0), stop=(k == DK - 1), skip_group_check=True)
            last.then_inc(logits_made, 1)

        for step in (turn_o, project_o, turn_xf, route):
            for t in range(FIRST):
                step(t)

        def count_tokens():
            pe.wait_ge(taken_ready, 1)
            pe.wait_ge(d_consts, 1)
            pe.wait_ge(logits_ready, TQ)
            mm_(bank[6][:, 0:E], upper[:, :], taken[:, :], start=True, stop=True)
            mm_(bank[7][:, 0:E], allones[:, :], taken[:, :], start=True, stop=True).then_inc(counts_made, 1)

        def hidden(g, u):
            n = SU * g + u
            wait(pe, hid_ready, n - 1)
            for w in range(2):
                for k in range(DK):
                    last = mm_(bank[2 * (u % 2) + w][:, :], w12s[:, k, w, u * P:(u + 1) * P],
                               xfT[:, k, bass.ds(g * GR, GR)], start=(k == 0), stop=(k == DK - 1))
            last.then_inc(hid_made, 1)

        def down(g, u):
            pe.wait_ge(hid_ready, SU * g + u + 1)
            if u == 0:
                wait(pe, ysh_added, g)
            for j in range(4):
                last = mm_(bank[4 + j // 2][:, (j % 2) * D:(j % 2 + 1) * D], gsh[:, u % 2, j * P:(j + 1) * P],
                           w3s[:, u, :], start=(u == 0 and j % 2 == 0), stop=(u == SU - 1), skip_group_check=True)
            if u == SU - 1:
                last.then_inc(ysh_made, 1)

        def shared(g):
            pe.wait_ge(xf_moved, 2 * g + 2)
            for u in range(SU):
                n = SU * g + u
                now, last = beside(n), beside(n - 2)
                if last is not None:
                    route(last)
                if now is not None:
                    turn_o(now)
                if n == COUNT_AT:
                    count_tokens()
                hidden(g, u)
                if now is not None:
                    project_o(now)
                if beside(n - 1) is not None:
                    turn_xf(beside(n - 1))
                if u:
                    down(g, u - 1)
            down(g, SU - 1)

        pe.wait_ge(ws_loaded, 48)
        for g in range(GB):
            shared(g)

        pe.wait_ge(wr_loaded, 16 * 3 * E)
        pe.wait_ge(ysh_added, GB)

        def turn_slot(s, i, c):
            pe.wait_ge(slot_loaded[c % 4], 16 * (i + c // 4 + 1))
            for k in range(DK):
                last = nc.tensor.transpose(bank[c % 2][:, k * P:(k + 1) * P], xsl[:, c % 4, k * P:(k + 1) * P],
                                           ident[:, :])
            last.then_inc(slot_turned, 1)

        def slot_hidden(s, p):
            e = nc.tensor.value_load(exps[0:1, bass.ds(s, 1)], min_val=0, max_val=E - 1)
            pe.wait_ge(slotT_ready, s + 1)
            wait(pe, rg_ready, s - 1)
            for k in range(DK):
                last = mm_(bank[2 + p][:, :], xsT[:, p, k, :], w12r[:, e, k, :],
                           start=(k == 0), stop=(k == DK - 1))
            last.then_inc(rh_made, 1)

        def turn_hidden(s, p):
            pe.wait_ge(rg_ready, s + 1)
            for k in range(2):
                last = nc.tensor.transpose(bank[4 + p][:, k * P:(k + 1) * P], rg[:, p, k * P:(k + 1) * P], ident[:, :])
            last.then_inc(rg_turned, 1)

        def slot_down(s, p):
            e = nc.tensor.value_load(exps[0:1, bass.ds(s, 1)], min_val=0, max_val=E - 1)
            pe.wait_ge(rgT_ready, s + 1)
            wait(pe, yo_ready, s - 1)
            for k in range(2):
                last = mm_(bank[6 + p][:, 0:D], rgT[:, p, k * P:(k + 1) * P], w3r[:, e, k, :],
                           start=(k == 0), stop=(k == 1))
            last.then_inc(ry_made, 1)

        def slot(s, i, c):
            if inside(s):
                slot_hidden(s, c % 2)
            if inside(s + 1):
                turn_slot(s + 1, i, c + 1)
            if inside(s - 1):
                turn_hidden(s - 1, (c + 1) % 2)
            if inside(s - 2):
                slot_down(s - 2, c % 2)

        turn_slot(0, 0, 0)
        slot_loop(pe, slot)

        pe.wait_ge(yo_ready, NS)
        for g in range(GB, NG):
            shared(g)

    @block.scalar
    def _(act):
        a = nc.scalar.activation
        act.wait_ge(eps_made, 1)

        def deviations(first):
            act.wait_ge(var_ready, first)
            a(sd[:, :, :], mv[:, :, 1:2], ACT.Sqrt, bias=eps[:, :]).then_inc(sd_ready, 1)

        def affine(n, c, kind):
            act.wait_ge(xt_turned, n + 1)
            wait(act, v_made, n - 1)
            for k in range(DK):
                last = a(xT[:, c, k, :], bank[c][:, k * P:(k + 1) * P], ACT.Identity,
                         scale=lnw[:, kind, 0, k:k + 1], bias=lnw[:, kind, 1, k:k + 1])
            last.then_inc(xT_ready, 1)

        def square(n, c, i):
            wait(act, ssq_ready, n)
            act.wait_ge((q_made, k_made)[i], n + 1)
            a(sq[:, i, :], bank[2 + 3 * c + i][:, :], ACT.Square).then_inc(sq_ready, 1)

        def keep_v(t, n, c):
            act.wait_ge(v_made, n + 1)
            a(vn[:, c * H:(c + 1) * H, t, 0:DH], bank[4 + 3 * c][:, :].rearrange("p (h d) -> p h d", d=DH),
              ACT.Copy).then_inc(v_used, 1)

        def norms(n):
            act.wait_ge(ssq_ready, n + 1)
            a(nrm[:, :], ssq[:, :], ACT.Sqrt).then_inc(nrm_ready, 1)

        deviations(1)
        deviations(2)
        act.wait_ge(consts_loaded, 16 * NC_CONST)
        for c in range(B):
            affine(c, c, 0)

        def stage_a(t):
            if not (isinstance(t, int) and t == 0):
                norms(2 * t - 1)
            last = isinstance(t, int) and t == TQ - 1
            deviations(2 * t + 3)
            square(2 * t, 0, 0)
            if not last:
                deviations(2 * t + 4)
            square(2 * t, 0, 1)
            keep_v(t, 2 * t, 0)
            norms(2 * t)
            square(2 * t + 1, 1, 0)
            square(2 * t + 1, 1, 1)
            for c in range(B):
                affine(2 * t + 2 + c, c, 1 if last else 0)
            keep_v(t, 2 * t + 1, 1)

        pair_loop(act, stage_a, TQ)
        norms(NT - 1)
        for c in range(B):
            square(NT + c, c, 1)
            keep_v(TQ, NT + c, c)
            norms(NT + c)

        act.wait_ge(masks_made, 1)
        act.wait_ge(zeros_made, 1)
        act.wait_ge(k_used, NT + B)

        def scale_head(hh, p, g):
            what, first, n = TURNS[g]
            act.wait_ge(heads_turned, NTURN * hh + g + 1)
            cols = slice(first * P, (first + n) * P)
            src = bank[TURN_BANK[g]]
            if what == "k":
                a(kT1[p][:, cols], src[:, 0:n * P], ACT.Copy, scale=qks[:, 1:2]).then_inc(scaled, 1)
            else:
                a(qT1[p][:, cols], src[:, 0:n * P], ACT.Copy, scale=qks[:, 0:1])
                a(qT2[p][0:DH, cols], src[0:DH, 0:n * P], ACT.Copy, scale=qks[0:DH, 0:1]).then_inc(scaled, 1)

        def keep_neg(hh, p):
            for z in range(2):
                act.wait_ge(neg_turned, 2 * hh + z + 1)
                a(qT2[p][DH:DH + 1, z * QC:(z + 1) * QC], bank[NEG_BANK[z]][DH:DH + 1, :],
                  ACT.Copy).then_inc(neg_row, 1)

        def exponentials(hh, p, s):
            act.wait_ge(scores_made, STEPS * hh + s + 1)
            wait(act, pv_done, STEPS * hh + s - 2)
            bias = mbias[p][:, :] if s % TK == TK - 1 else zero[:, :]
            a(prob[:, s % 3, :], bank[s % 2][:, :], ACT.Exp, bias=bias).then_inc(probs_ready, 1)

        for g in range(NTURN):
            scale_head(0, 0, g)
        keep_neg(0, 0)

        def stage_b(hh, p, prepare):
            for s in range(STEPS):
                exponentials(hh, p, s)
                if prepare and s < NTURN:
                    scale_head(hh + 1, 1 - p, s)
            if prepare:
                keep_neg(hh + 1, 1 - p)

        head_loop(act, stage_b)


        def copy_oT(t):
            for i, c in enumerate((1, 0)):
                act.wait_ge(o_turned, 2 * t + i + 1)
                a(oT[:, t % 2, c, :], cbanks(t)[c][:, :], ACT.Copy).then_inc(oT_ready, 1)

        def copy_xfT(t):
            act.wait_ge(xf_turned, t + 1)
            src = cbanks(t)[1][:, :].rearrange("p (c k n) -> p k c n", c=B, k=DK)
            dst = xfT[:, :, 2 * t * P:(2 * t + 2) * P].rearrange("p k (c n) -> p k c n", c=B)
            a(dst, src, ACT.Copy).then_inc(xf_moved, 1)

        def copy_logits(t):
            act.wait_ge(logits_made, t + 1)
            a(logits[:, 2 * t:2 * t + 2, :], cbanks(t)[0][:, 0:2 * E].rearrange("p (c e) -> p c e", c=B),
              ACT.Copy).then_inc(logits_ready, 1)

        for step in (copy_oT, copy_xfT, copy_logits):
            for t in range(FIRST):
                step(t)

        def shared(g):
            for u in range(SU):
                n = SU * g + u
                now, last = beside(n), beside(n - 2)
                if last is not None:
                    copy_logits(last)
                    if last == TQ - 1:
                        act.drain()
                        a(score[:, :, :], logits[:, :, :], ACT.Sigmoid).then_inc(score_ready, 1)
                if now is not None:
                    copy_oT(now)
                act.wait_ge(hid_made, n + 1)
                wait(act, hid_ready, n - 1)
                a(sil[:, u % 2, :], bank[2 * (u % 2)][:, :], ACT.Silu).then_inc(sil_ready, 1)
                if beside(n - 1) is not None:
                    copy_xfT(beside(n - 1))

        for g in range(GB):
            shared(g)

        def copy_slotT(s, p):
            act.wait_ge(slot_turned, s + 1)
            a(xsT[:, p, :, :], bank[p][:, 0:D].rearrange("p (k n) -> p k n", k=DK), ACT.Copy).then_inc(slotT_ready, 1)

        def slot_silu(s, p):
            act.wait_ge(rh_made, s + 1)
            wait(act, rg_ready, s - 1)
            a(sil[:, p, 0:HID], bank[2 + p][:, 0:HID], ACT.Silu).then_inc(rsil_ready, 1)

        def copy_result(s, p, before):
            act.wait_ge(ry_made, s + 1)
            wait(act, yo_stored[p], 16 * before)
            a(yo[:, p, :], bank[6 + p][:, 0:D], ACT.Copy).then_inc(yo_ready, 1)

        def slot(s, i, c):
            if inside(s):
                slot_silu(s, c % 2)
            if inside(s + 1):
                copy_slotT(s + 1, (c + 1) % 2)
            if inside(s - 2):
                copy_result(s - 2, c % 2, 2 * i + (c - 2) // 2)

        copy_slotT(0, 0)
        slot_loop(act, slot)

        for g in range(GB, NG):
            shared(g)

    @block.vector
    def _(dve):
        v = nc.vector

        def moments(src, made):
            for c in range(B):
                v.bn_stats(st[:, c, :], src(c))
            v.drain()
            for c in range(B):
                last = v.bn_aggr(mv[:, c, :], st[:, c, :])
            last.then_inc(made, 1)

        def normalise(dst, src, done=None):
            v.reciprocal(rs[:, :, :], sd[:, :, :])
            v.drain()
            for c in range(B):
                last = v.tensor_scalar(dst(c), src(c), mv[:, c, 0:1], rs[:, c, :], ALU.subtract, ALU.mult)
            if done is not None:
                last.then_inc(done, 1)
            v.drain()

        def norm_pair(t, kind):
            dve.wait_ge(x_loaded, 32 * (t + 1) + (32 if kind else 0))
            xin_ = lambda c: xin[:, c, :]
            moments(xin_, var_ready)
            dve.wait_ge(sd_ready, 2 * t + 1)
            if kind:
                wait(dve, xt_turned, 2 * t)
                normalise(lambda c: xn2[:, c, :], xin_, xnorm_ready)
                return
            normalise(lambda c: xn[:, c, :], xin_, x_used)
            moments(lambda c: xn[:, c, :], var_ready)
            dve.wait_ge(sd_ready, 2 * t + 2)
            wait(dve, xt_turned, 2 * t)
            normalise(lambda c: xn2[:, c, :], lambda c: xn[:, c, :], xnorm_ready)

        def l2norm(t, n, c, latent, sq_at):
            parts = ((0, q_used, on), (1, k_used, kn)) if latent else ((1, k_used, kn),)
            for j, (i, _, _) in enumerate(parts):
                dve.wait_ge(sq_ready, sq_at + j + 1)
                last = v.tensor_reduce(ssq[:, i * H:(i + 1) * H], sq[:, i, :].rearrange("p (h d) -> p h d", d=DH),
                                       AX.X, ALU.add)
            last.then_inc(ssq_ready, 1)
            dve.wait_ge(nrm_ready, n + 1)
            v.tensor_scalar(rnr[:, :], nrm[:, :], L2_EPS, None, ALU.max)
            v.drain()
            v.reciprocal(rnr[:, :], rnr[:, :])
            v.drain()
            for i, used, dst in parts:
                rows = dst[:, t, c * H:(c + 1) * H, :] if i == 0 else dst[:, c * H:(c + 1) * H, t, :]
                v.tensor_tensor(rows, bank[2 + 3 * c + i][:, :].rearrange("p (h d) -> p h d", d=DH),
                                rnr[:, i * H:(i + 1) * H].unsqueeze(2).to_broadcast([P, H, DH]),
                                ALU.mult).then_inc(used, 1)
            v.drain()

        norm_pair(0, 0)

        def stage_a(t):
            if not (isinstance(t, int) and t == 0):
                l2norm(t - 1, 2 * t - 1, 1, True, 2 * (2 * t - 1))
            norm_pair(t + 1, 1 if isinstance(t, int) and t == TQ - 1 else 0)
            l2norm(t, 2 * t, 0, True, 2 * (2 * t))

        pair_loop(dve, stage_a, TQ)
        l2norm(TQ - 1, NT - 1, 1, True, 2 * (NT - 1))
        for c in range(B):
            l2norm(TQ, NT + c, c, False, 2 * NT + c)

        dve.wait_ge(masks_made, 1)

        def split_head(hh, p, g):
            what, first, n = TURNS[g]
            cols = slice(first * P, (first + n) * P)
            src = bank[TURN_BANK[g]]
            dve.wait_ge(scaled, NTURN * hh + g + 1)
            if what == "k":
                v.scalar_tensor_tensor(kT2[p][0:DH, cols], src[0:DH, 0:n * P], qks[0:DH, 1:2], kT1[p][0:DH, cols],
                                       ALU.mult, ALU.subtract).then_inc(split, 1)
            else:
                v.scalar_tensor_tensor(qT1[p][DH:P, cols], src[DH:P, 0:n * P], qks[DH:P, 0:1], qT1[p][DH:P, cols],
                                       ALU.mult, ALU.subtract).then_inc(split, 1)

        def reduce_piece(hh, k):
            tile, c = divmod(k, len(PIECES))
            dve.wait_ge(piece_made, NP_ * hh + k + 1)
            v.tensor_reduce(mx[:, tile, c:c + 1], bank[2 + k % 2][:, 0:PIECES[c][1]], AX.X, ALU.max)\
                .then_inc(piece_used, 1)

        def negate(hh, p):
            v.tensor_scalar(mbias[p][:, :], maskf[:, bass.ds(hh, 1)], 0.0, None, ALU.add)
            v.drain()
            v.tensor_reduce(mm[:, :], mx[:, :, :], AX.X, ALU.max)
            v.drain()
            wait(dve, neg_turned, 2 * hh)
            v.tensor_scalar(zneg[:, :, DH], mm[:, :], -1.0, None, ALU.mult).then_inc(neg_ready, 1)

        def divide(hh, c):
            dve.wait_ge(pv_done, STEPS * hh + TK * (c + 1))
            sums = bank[4 + c][:, 0:4 * (DH + 1)].rearrange("p (j d) -> p j d", d=DH + 1)
            v.reciprocal(rec[:, c, :], sums[:, :, DH])
            v.drain()
            v.tensor_tensor(on[:, 4 * c:4 * c + 4, hh, :], sums[:, :, 0:DH],
                            rec[:, c, :].unsqueeze(2).to_broadcast([P, 4, DH]), ALU.mult).then_inc(o_ready, 1)

        for g in range(NTURN):
            split_head(0, 0, g)
        for k in range(NP_):
            reduce_piece(0, k)
        negate(0, 0)

        def stage_b(hh, p, prepare):
            for s in range(STEPS):
                if prepare and s < NTURN:
                    split_head(hh + 1, 1 - p, s)
                if prepare:
                    for k in piece_steps.get(s, ()):
                        reduce_piece(hh + 1, k)
                if s == TK:
                    divide(hh, 0)
            if prepare:
                negate(hh + 1, 1 - p)
            divide(hh, 1)

        head_loop(dve, stage_b)

        v.drain()
        dve.wait_ge(c_loaded, 64)

        def product(g, u):
            n = SU * g + u
            dve.wait_ge(sil_ready, n + 1)
            v.tensor_tensor(gsh[:, u % 2, :], sil[:, u % 2, :], bank[2 * (u % 2) + 1][:, :], ALU.mult).then_inc(hid_ready, 1)

        def add_shared(g):
            dve.wait_ge(ysh_made, g + 1)
            for j in range(2):
                rows = x2[:, 4 * g + 2 * j:4 * g + 2 * j + 2, :]
                last = v.tensor_tensor(rows, bank[4 + j][:, :].rearrange("p (c d) -> p c d", c=2), rows, ALU.add)
            last.then_inc(ysh_added, 1)
            v.drain()

        def stage_c(t):
            def variances(src):
                for c in range(B):
                    v.bn_stats(st[:, c, :], src(c))
                v.drain()
                for c in range(B):
                    last = v.bn_aggr(mv[:, c, :], st[:, c, :])
                last.then_inc(cvar_ready, 1)
                v.drain()

            y = lambda c: cbanks(t)[0][:, c * D:(c + 1) * D]
            dve.wait_ge(y_made, t + 1)
            variances(y)
            for c in range(B):
                last = v.scalar_tensor_tensor(yn[:, c, :], y(c), mv[:, c, 0:1], lno[:, 0, :], ALU.subtract, ALU.mult)
            last.then_inc(y_used, 1)
            v.drain()
            dve.wait_ge(xres_ready, t + 1)
            dve.wait_ge(crs_ready, 2 * t + 1)
            for c in range(B):
                last = v.scalar_tensor_tensor(x2[:, 2 * t + c, :], yn[:, c, :], rs[:, c, :], xres[:, t % 2, c, :],
                                              ALU.mult, ALU.add)
            last.then_inc(xres_used, 1)
            v.drain()
            variances(lambda c: x2[:, 2 * t + c, :])
            dve.wait_ge(crs_ready, 2 * t + 2)
            for c in range(B):
                last = v.tensor_scalar(xf[:, 2 * t + c, :], x2[:, 2 * t + c, :], mv[:, c, 0:1], rs[:, c, :],
                                       ALU.subtract, ALU.mult)
            last.then_inc(xf_ready, 1)

        for t in range(FIRST):
            stage_c(t)
        hid = 0

        def shared_product():
            nonlocal hid
            product(hid // SU, hid % SU)
            hid += 1
            if hid % SU == 1 and hid > 1:
                add_shared(hid // SU - 1)

        while beside(hid) is not None:
            shared_product()
            stage_c(beside(hid - 1))
            shared_product()

        dve.wait_ge(score_ready, 1)
        dve.wait_ge(d_consts, 1)

        def over_tiles(ap):
            return ap.unsqueeze(1).to_broadcast([P, NT, E])

        def over_experts(ap):
            return ap.unsqueeze(2).to_broadcast([P, NT, E])

        v.tensor_tensor(sel[:, :, :], score[:, :, :], over_tiles(ebias[:, :]), ALU.add)
        v.drain()
        for k in range(TOP):
            v.tensor_reduce(best[:, :], sel[:, :, :], AX.X, ALU.max)
            v.drain()
            v.tensor_tensor(work[0][:, :, :], sel[:, :, :], over_experts(best[:, :]), ALU.is_equal)
            v.drain()
            v.tensor_tensor(work[0][:, :, :], work[0][:, :, :], over_tiles(number[:, :]), ALU.mult)
            v.drain()
            shared_product()
            v.tensor_reduce(best[:, :], work[0][:, :, :], AX.X, ALU.min)
            v.drain()
            v.tensor_tensor(onehot[k][:, :, :], over_tiles(number[:, :]), over_experts(best[:, :]), ALU.is_equal)
            v.drain()
            if k < TOP - 1:
                v.scalar_tensor_tensor(sel[:, :, :], onehot[k][:, :, :], MASKED, sel[:, :, :], ALU.mult, ALU.add)
            v.tensor_tensor(work[0][:, :, :], onehot[k][:, :, :], score[:, :, :], ALU.mult)
            v.drain()
            v.tensor_reduce(gate[:, :, k], work[0][:, :, :], AX.X, ALU.add)
            v.drain()
            shared_product()
        v.tensor_tensor(work[0][:, :, :], onehot[0][:, :, :], onehot[1][:, :, :], ALU.add)
        v.drain()
        v.tensor_reduce(taken[:, :], work[0][:, :, :].rearrange("p n e -> p e n"), AX.X, ALU.add).then_inc(taken_ready, 1)
        v.memset(work[1][:, 0:1, :], 0.0)
        v.tensor_copy(work[1][:, 1:NT, :], work[0][:, 0:NT - 1, :])
        v.drain()
        src, step = 1, 1
        while step < NT:
            v.tensor_copy(work[1 - src][:, 0:step, :], work[src][:, 0:step, :])
            v.tensor_tensor(work[1 - src][:, step:NT, :], work[src][:, step:NT, :], work[src][:, 0:NT - step, :], ALU.add)
            v.drain()
            src, step = 1 - src, 2 * step
        before = work[src]
        shared_product()
        dve.wait_ge(counts_made, 1)
        v.tensor_scalar(tiles_f[:, :], bank[7][:, 0:E], float(P - 1), None, ALU.add)
        v.drain()
        v.tensor_copy(tiles_i[:, :], tiles_f[:, :])
        v.drain()
        v.tensor_scalar(tiles_i[:, :], tiles_i[:, :], P.bit_length() - 1, None, ALU.logical_shift_right)
        v.drain()
        v.tensor_copy(tiles_f[:, :], tiles_i[:, :])
        v.drain()
        v.tensor_copy(ends[0][:, :], tiles_f[:, :])
        v.drain()
        src, step = 0, 1
        while step < E:
            v.tensor_copy(ends[1 - src][:, 0:step], ends[src][:, 0:step])
            v.tensor_tensor(ends[1 - src][:, step:E], ends[src][:, step:E], ends[src][:, 0:E - step], ALU.add)
            v.drain()
            src, step = 1 - src, 2 * step
        end = ends[src]
        shared_product()
        v.tensor_tensor(offs[:, :], end[:, :], tiles_f[:, :], ALU.subtract)
        v.drain()
        v.tensor_scalar(offs[:, :], offs[:, :], float(P), None, ALU.mult)
        v.drain()
        v.tensor_tensor(offs[:, :], offs[:, :], bank[6][:, 0:E], ALU.add)
        v.drain()
        v.tensor_tensor(before[:, :, :], before[:, :, :], over_tiles(offs[:, :]), ALU.add)
        v.drain()
        for k in range(TOP):
            v.tensor_tensor(sel[:, :, :], onehot[k][:, :, :], before[:, :, :], ALU.mult)
            v.drain()
            v.tensor_reduce(posf[:, :], sel[:, :, :], AX.X, ALU.add)
            v.drain()
            v.tensor_copy(posi[:, :, k], posf[:, :])
            v.drain()
            if k == 0:
                shared_product()
        v.tensor_tensor(passed[:, :, :], end[0:1, :].unsqueeze(1).to_broadcast([1, NS + 1, E]),
                        slot_f[:, :].unsqueeze(2).to_broadcast([1, NS + 1, E]), ALU.is_le)
        v.drain()
        v.tensor_reduce(passed_sum[:, :], passed[:, :, :], AX.X, ALU.add)
        v.drain()
        v.tensor_scalar(passed_sum[:, :], passed_sum[:, :], float(E - 1), None, ALU.min)
        v.drain()
        v.tensor_copy(exps[0:1, :], passed_sum[:, :])
        v.drain().then_inc(routed, 1)

        while hid < SU * GB:
            shared_product()
        add_shared(GB - 1)

        def slot_product(s, p):
            dve.wait_ge(rsil_ready, s + 1)
            wait(dve, rg_turned, s - 1)
            v.tensor_tensor(rg[:, p, :], sil[:, p, 0:HID], bank[2 + p][:, HID:], ALU.mult).then_inc(rg_ready, 1)

        def copy_hidT(s, p):
            dve.wait_ge(rg_turned, s + 1)
            wait(dve, ry_made, s - 1)
            v.tensor_copy(rgT[:, p, :], bank[4 + p][:, 0:HID]).then_inc(rgT_ready, 1)

        def slot(s, i, c):
            if inside(s - 1):
                copy_hidT(s - 1, (c + 1) % 2)
            if inside(s):
                slot_product(s, c % 2)

        slot_loop(dve, slot)

        def combine(n):
            dve.wait_ge(gathered[n % 4], 32 * (n // 4 + 1))
            for k in range(TOP):
                last = v.scalar_tensor_tensor(x2[:, n, :], gat[n % 4][:, k, :], gate[:, n, k:k + 1], x2[:, n, :],
                                              ALU.mult, ALU.add)
                if k < TOP - 1:
                    v.drain()
            last.then_inc(combined, 1)

        done = 0
        for g in range(GB, NG):
            for u in range(SU):
                product(g, u)
                for _ in range(2 if u else 0):
                    if done < 4 * g:
                        combine(done)
                        done += 1
            add_shared(g)
        while done < NT:
            combine(done)
            done += 1

    es.close()


_INS = ["x", "ctx_1024", "mask_BxS2_bk0", "L0_xattn_ln_x_w", "L0_xattn_ln_x_b", "L0_xattn_ln_l_w",
        "L0_xattn_ln_l_b", "L0_xattn_Wq", "L0_xattn_Wkv", "L0_xattn_q_scale", "L0_xattn_k_scale",
        "L0_xattn_Wo", "L0_xattn_ln_o_w", "L0_xattn_ln_o_b", "L0_ffn_router_w", "L0_ffn_expert_bias",
        "L0_ffn_shared_w1", "L0_ffn_shared_w2", "L0_ffn_shared_w3", "L0_ffn_routed_w1",
        "L0_ffn_routed_w2", "L0_ffn_routed_w3"]


def kernel(**inputs):
    import numpy as np
    import concourse.bacc as bacc
    from concourse.bass_utils import run_bass_kernel_spmd

    nc = bacc.Bacc("TRN2", target_bir_lowering=False, num_devices=1)
    arrays, args = {}, []
    for name in _INS:
        a = np.ascontiguousarray(inputs[name])
        if a.dtype == np.bool_:
            a = a.astype(np.int32)
        arrays[f"in_{name}"] = a
        args.append(nc.dram_tensor(f"in_{name}", a.shape, mybir.dt.from_np(a.dtype), kind="ExternalInput").ap())
    out = nc.dram_tensor("out", (B, S, D), F32, kind="ExternalOutput").ap()
    build(nc, *args, out)
    r = run_bass_kernel_spmd(nc, [arrays], core_ids=[0])
    return r.results[0]["out"]
```

```python
from contextlib import ExitStack

import concourse.bass as bass
from concourse import mybir

F32 = mybir.dt.float32
F32R = mybir.dt.float32r
I32 = mybir.dt.int32
ACT = mybir.ActivationFunctionType
ALU = mybir.AluOpType
AX = mybir.AxisListType

B, S, D = 2, 1024, 256
M = 64
H, DH = 8, 64
INNER = H * DH
P = 128
DK = D // P
TQ = S // P
TK = TQ + 1
NT = B * TQ
BH = B * H
QC = 512
CH = S // QC
STEPS = CH * TK
SCALE = 8.0
LN_EPS, L2_EPS = 1e-5, 1e-12
MASKED = -1e30
E, HID = 16, 256
SH = 1024
SU = SH // P
GR = 512
NG = NT * P // GR
TOP = 2
NS = (TOP * NT * P + E * (P - 1)) // P
NGAT = 3
FAR = 99.0
KEYS = S + M
PIECES = [(0, 384), (384, 384), (768, KEYS - 768)]
NP_ = len(PIECES) * TQ


def wait(eng, sem, value):
    if isinstance(value, int) and value <= 0:
        return
    eng.wait_ge(sem, value)


def build(nc, x, ctx, mask, ln_x_w, ln_x_b, ln_l_w, ln_l_b, wq, wkv, q_scale, k_scale, wo,
          ln_o_w, ln_o_b, router_w, expert_bias, sw1, sw2, sw3, rw1, rw2, rw3, out, dbg=None):
    es = ExitStack()

    def sb(name, shape, dt=F32, stack=es):
        return stack.enter_context(nc.sbuf_tensor(name, shape, dt))

    def sem(name):
        return es.enter_context(nc.semaphore(name))

    xs_dram = nc.dram_tensor("slot_rows", (NS * P, D), F32, kind="Internal").ap()
    ys_dram = nc.dram_tensor("slot_results", (NS * P, D), F32, kind="Internal").ap()

    ident = sb("ident", [P, P])
    half = sb("half", [P, 2, 1])
    eps = sb("eps", [P, 2, 1])
    zero = sb("zero", [P, 1])
    zrow = sb("zrow", [P, D])
    lnw = sb("lnw", [P, 2, 2, DK])
    qks = sb("qks", [P, 2])
    maskf = sb("maskf", [P, BH])
    mask_i = sb("mask_i", [M, B], I32)
    maskrow_i = sb("maskrow_i", [1, B, M], I32)
    wr = sb("wr", [P, DK, E])
    ebias = sb("ebias", [P, E])
    exps = sb("exps", [P, NS + 1], I32)
    posi = sb("posi", [P, NT, TOP], I32)
    gate = sb("gate", [P, NT, TOP])
    st = sb("st", [P, 2, 6])
    mv = sb("mv", [P, 2, 2])
    sd = sb("sd", [P, 2, 1])
    rs = sb("rs", [P, 2, 1])

    first = ExitStack()
    wqkv = sb("wqkv", [P, DK, 3 * INNER], stack=first)
    xin = sb("xin", [P, 2, D], stack=first)
    xn = sb("xn", [P, 2, D], stack=first)
    xn2 = sb("xn2", [P, 2, D], stack=first)
    xT = sb("xT", [P, 2, DK, P], stack=first)
    sq = sb("sq", [P, 2, INNER], stack=first)
    ssq = sb("ssq", [P, 2 * H], stack=first)
    nrm = sb("nrm", [P, 2 * H], stack=first)
    rnr = sb("rnr", [P, 2 * H], stack=first)
    first_end = nc.sbuf_bytes_remaining
    first.close()
    moe = ExitStack()
    xsl = sb("xsl", [P, 4, D], stack=moe)
    xsT = sb("xsT", [P, 2, DK, P], stack=moe)
    w_slot = sb("w_slot", [P, 2, DK, 2 * HID], stack=moe)
    rgT = sb("rgT", [P, 2, HID], stack=moe)
    yo = sb("yo", [P, 2, D], stack=moe)
    gat = [sb(f"slot_result{i}", [P, TOP, D], stack=moe) for i in range(NGAT)]
    moe.close()
    cst = ExitStack()
    wo_sb = sb("wo_sb", [P, INNER // P, D], stack=cst)
    lno = sb("lno", [P, 2, D], stack=cst)
    xres = sb("xres", [P, 2, 2, D], stack=cst)
    oT = sb("oT", [P, 2, 2, INNER], stack=cst)
    yn = sb("yn", [P, 2, D], stack=cst)
    cst.enter_context(nc.sbuf_tensor("rest_of_first", [P, (nc.sbuf_bytes_remaining - first_end) // 4], F32))

    att = ExitStack()
    on = sb("on", [P, TQ, BH, DH], stack=att)
    kn = sb("kn", [P, BH, TK, DH], stack=att)
    vn = sb("vn", [P, BH, TK, DH + 1], stack=att)
    tiles = sb("tiles", [P, TK + 1 + TQ, DH], stack=att)
    qT1 = [sb(f"q_hi_lo{i}", [P, S], F32R, att) for i in range(2)]
    qT2 = [sb(f"q_hi_max{i}", [P, S], F32R, att) for i in range(2)]
    kT1 = [sb(f"k_hi_hi{i}", [P, TK * P], F32R, att) for i in range(2)]
    kT2 = [sb(f"k_lo_one{i}", [P, TK * P], F32R, att) for i in range(2)]
    prob = sb("prob", [P, 3, QC], stack=att)
    mx = sb("mx", [P, TQ, len(PIECES)], stack=att)
    mbias = [sb(f"mbias{i}", [P, 1], stack=att) for i in range(2)]
    mm = sb("mm", [P, TQ], stack=att)
    zneg = sb("zneg", [P, DH + TQ], stack=att)
    own_tile = sb("own_tile", [P, TQ], stack=att)
    rec = sb("rec", [P, 2, QC // P], stack=att)
    maskrow = sb("maskrow", [P, BH, M], F32R, att)
    firstrow = sb("firstrow", [P, P], F32R, att)
    att.close()

    ffn = ExitStack()
    w3r = sb("w3r", [P, E, HID // P, D], stack=ffn)
    x2 = sb("x2", [P, NT, D], stack=ffn)
    xf = sb("xf", [P, NT, D], stack=ffn)
    xfT = sb("xfT", [P, DK, NT * P], stack=ffn)
    w12r = sb("w12r", [P, E, DK, 2 * HID], stack=ffn)
    w12s = sb("w12s", [P, DK, 2, SH], stack=ffn)
    w3s = sb("w3s", [P, SU, D], stack=ffn)


    sil = sb("sil", [P, 2, GR], stack=ffn)
    gsh = sb("gsh", [P, 2, GR], stack=ffn)
    ffn.close()
    rt = ExitStack()
    rt.enter_context(nc.sbuf_tensor("below_routing", [P, (B * H * TQ * DH) + 3 * NT * D], F32))
    below_bytes = nc.sbuf_bytes_remaining
    onehot = [sb(f"onehot{k}", [P, NT, E], stack=rt) for k in range(TOP)]
    logits = sb("logits", [E, NT * P], stack=rt)
    score = sb("score", [P, NT, E], stack=rt)
    sel = sb("sel", [P, NT, E], stack=rt)
    work = [sb(f"work{k}", [P, NT, E], stack=rt) for k in range(2)]
    best = sb("best", [P, NT], stack=rt)
    number = sb("number", [P, E], stack=rt)
    number_i = sb("number_i", [P, E], I32, rt)
    slot_i = sb("slot_i", [1, NS + 1], I32, rt)
    slot_f = sb("slot_f", [1, NS + 1], stack=rt)
    passed = sb("passed", [1, NS + 1, E], stack=rt)
    passed_sum = sb("passed_sum", [1, NS + 1], stack=rt)
    upper = sb("upper", [P, P], stack=rt)
    allones = sb("allones", [P, P], stack=rt)
    taken = sb("taken", [P, E], stack=rt)
    tiles_i = sb("tiles_i", [P, E], I32, rt)
    tiles_f = sb("tiles_f", [P, E], stack=rt)
    ends = [sb(f"ends{k}", [P, E], stack=rt) for k in range(2)]
    offs = sb("offs", [P, E], stack=rt)
    posf = sb("posf", [P, NT], stack=rt)
    rt_bytes = below_bytes - nc.sbuf_bytes_remaining
    OVER_D = -(-rt_bytes // (4 * DK * 2 * HID))
    rt.close()
    cst.close()

    bank = [es.enter_context(nc.psum_tensor(f"bank{i}", [P, 512], F32)) for i in range(8)]

    ident_made, ln_loaded, w_loaded = sem("ident_made"), sem("ln_weights_loaded"), sem("projections_loaded")
    consts_loaded, consts_made, masks_made = sem("consts_loaded"), sem("consts_made"), sem("masks_made")
    xs_zeroed = sem("xs_zeroed")
    x_loaded, x_used, var_ready, rs_ready = sem("x_loaded"), sem("x_used"), sem("var_ready"), sem("rs_ready")
    xnorm_ready, xt_turned, xT_ready = sem("xnorm_ready"), sem("xt_turned"), sem("xT_ready")
    q_made, k_made, v_made = sem("q_made"), sem("k_made"), sem("v_made")
    sq_ready, ssq_ready, nrm_ready = sem("sq_ready"), sem("ssq_ready"), sem("nrm_ready")
    q_used, k_used, v_used = sem("q_used"), sem("k_used"), sem("v_used")
    collected, heads_turned, scaled, split = sem("collected"), sem("heads_turned"), sem("scaled"), sem("split")
    piece_made, piece_used = sem("piece_made"), sem("piece_used")
    neg_ready, neg_turned, neg_row = sem("neg_ready"), sem("neg_turned"), sem("neg_row")
    scores_made, probs_ready, pv_done = sem("scores_made"), sem("probs_ready"), sem("pv_done")
    o_ready = sem("o_ready")
    c_loaded, xres_ready, xres_used = sem("c_loaded"), sem("xres_ready"), sem("xres_used")
    xres_loaded = [sem(f"xres_loaded{i}") for i in range(2)]
    o_turned, oT_ready = sem("o_turned"), sem("oT_ready")
    y_made, y_used, cvar_ready, crs_ready = sem("y_made"), sem("y_used"), sem("cvar_ready"), sem("crs_ready")
    xf_ready, xf_turned, xf_moved = sem("xf_ready"), sem("xf_turned"), sem("xf_moved")
    logits_made, logits_ready, logits_turned = sem("logits_made"), sem("logits_ready"), sem("logits_turned")
    d_consts, score_ready, taken_ready, counts_made, routed = (sem("d_consts"), sem("score_ready"),
                                                              sem("taken_ready"), sem("counts_made"), sem("routed"))
    placed, gates_ready, scattered = sem("placed"), sem("gates_ready"), sem("scattered")
    ws_loaded, wr_loaded = sem("shared_weights_loaded"), sem("routed_weights_loaded")
    hid_made, sil_ready, hid_ready, ysh_made, ysh_added = (sem("hid_made"), sem("sil_ready"), sem("hid_ready"),
                                                         sem("ysh_made"), sem("ysh_added"))
    slot_loaded = [sem(f"slot_loaded{i}") for i in range(4)]
    slot_turned, slotT_ready, w_placed, rh_made = (sem("slot_turned"), sem("slotT_ready"), sem("w_placed"),
                                                   sem("rh_made"))
    rsil_ready, rg_ready, ry_made, yo_ready = sem("rsil_ready"), sem("rg_ready"), sem("ry_made"), sem("yo_ready")
    yo_stored = [sem(f"yo_stored{i}") for i in range(2)]
    gathered = [sem(f"gathered{i}") for i in range(NGAT)]
    combined, out_stored = sem("combined"), sem("out_stored")

    NC_CONST = 8

    def pair_loop(eng, body, n):
        body(0)
        with eng.Fori(1, n - 1) as t:
            body(t)
        body(n - 1)

    def head_loop(eng, body):
        body(0, 0, True)
        body(1, 1, True)
        with eng.Fori(1, BH // 2 - 1) as i:
            body(2 * i, 0, True)
            body(2 * i + 1, 1, True)
        body(BH - 2, 0, True)
        body(BH - 1, 1, False)

    def inside(s):
        return not isinstance(s, int) or 0 <= s < NS

    def slot_loop(eng, body):
        for c in range(4):
            body(c, 0, c)
        with eng.Fori(1, NS // 4) as i:
            for c in range(4):
                body(4 * i + c, i, c)
        for s in range(NS // 4 * 4, NS + 1):
            body(s, s // 4, s % 4)

    piece_steps, at = {}, 0
    for s in range(5, 16):
        n = 3 if s in (8, 12) else 2
        piece_steps[s] = range(at, at + n)
        at += n
    assert at == NP_
    PREPARE_BANKS = (2, 3, 0, 1, 4, 5)
    TURNS = (("k", 0, TQ // 2, 6), ("q", TQ + 2, TQ // 2, 7), ("ctx", TQ, 1, 6))
    NTURN = len(TURNS)
    TURN_AT = {0: 0, 1: 1, 3: 2}
    PARTS = ("k even", "k odd", "q even", "q odd", "ctx")
    ROUND_AT = {0: "k even", 1: "k odd", 2: "q even", 3: "q odd", 4: "ctx"}
    REST_AT = {1: ("k even",), 2: ("k odd",), 3: ("q even",), 4: ("q odd", "ctx")}
    NEG_BANK = 7

    def part(hh, what):
        return len(PARTS) * hh + PARTS.index(what) + 1

    def tiles_of(buf, rows, odd):
        cols = buf[rows, 0:TQ * P].rearrange("p (i a n) -> p i a n", a=2, n=P)
        return cols[:, :, odd, :]

    def turned(b, rows):
        return bank[b][rows, :].rearrange("p (i n) -> p i n", n=P)

    LOW, HIGH = slice(0, DH), slice(DH, P)

    GB = NG - 1
    FIRST = 2
    EARLY = FIRST

    COUNT_AT = 15

    def beside(n):
        t = FIRST + n // 2
        return t if n >= 0 and n % 2 == 0 and t < TQ else None

    def cbanks(t, late=False):
        i = 4 if t == 0 else 2 if t == EARLY and not late else 6
        return bank[i], bank[i + 1]

    block = es.enter_context(nc.Block())

    @block.sync
    def _(sp):
        c = consts_loaded
        def load_x(t, kind):
            wait(sp, x_used, t)
            for b in range(B):
                if kind == "latent":
                    sp.dma_start(xin[:, b, :], x[b, bass.ds(t * P, P), :]).then_inc(x_loaded, 16)
                else:
                    for r in range(P // M):
                        sp.dma_start(xin[r * M:(r + 1) * M, b, :], ctx[b, :, :]).then_inc(x_loaded, 16)

        load_x(0, "latent")
        for k in range(DK):
            sp.dma_start(wqkv[:, k, 0:INNER], wq[k * P:(k + 1) * P, :]).then_inc(w_loaded, 16)
            sp.dma_start(wqkv[:, k, INNER:], wkv[k * P:(k + 1) * P, :]).then_inc(w_loaded, 16)
        for r in range(2):
            sp.dma_start(qks[r * DH:(r + 1) * DH, 0:1], q_scale.rearrange("(p a) -> p a", a=1)).then_inc(c, 16)
            sp.dma_start(qks[r * DH:(r + 1) * DH, 1:2], k_scale.rearrange("(p a) -> p a", a=1)).then_inc(c, 16)
        for b in range(B):
            sp.dma_start(mask_i[:, b:b + 1], mask[b, :].rearrange("(m a) -> m a", a=1)).then_inc(c, 16)
        sp.dma_start(maskrow_i[:, :, :], mask.rearrange("(a b) m -> a b m", a=1)).then_inc(c, 16)
        sp.dma_start(wr[:, :, :], router_w.rearrange("(k p) e -> p k e", p=P)).then_inc(c, 16)
        with sp.Fori(1, TQ) as t:
            load_x(t, "latent")
        load_x(TQ, "context")

        sp.wait_ge(masks_made, 1)
        for s in range(NS):
            sp.dma_start(xs_dram[s * P:(s + 1) * P, :], zrow[:, :]).then_inc(xs_zeroed, 16)

        sp.wait_ge(q_used, NT)
        sp.wait_ge(k_used, NT + B)
        sp.wait_ge(v_used, NT + B)
        sp.dma_start(wo_sb[:, :, :], wo.rearrange("(k p) d -> p k d", p=P)).then_inc(c_loaded, 16)
        sp.dma_start(lno[:, 0, :], ln_o_w.rearrange("(a d) -> a d", a=1).to_broadcast([P, D])).then_inc(c_loaded, 16)
        sp.dma_start(lno[:, 1, :], ln_o_b.rearrange("(a d) -> a d", a=1).to_broadcast([P, D])).then_inc(c_loaded, 16)
        sp.dma_start(ebias[:, :], expert_bias.rearrange("(a d) -> a d", a=1).to_broadcast([P, E])).then_inc(c_loaded, 16)

        def load_res(t):
            wait(sp, xres_used, t - 1)
            for b in range(B):
                sp.dma_start(xres[:, t % 2, b, :], x[b, bass.ds(t * P, P), :]).then_inc(xres_loaded[t % 2], 16)

        load_res(0)
        load_res(1)
        sp.wait_ge(o_ready, CH * BH)
        sp.wait_ge(split, len(PARTS) * BH)
        for w, src in enumerate((sw1, sw2)):
            sp.dma_start(w12s[:, :, w, :], src[0].rearrange("(k p) h -> p k h", p=P)).then_inc(ws_loaded, 16)
        sp.dma_start(w3s[:, :, :], sw3[0].rearrange("(u p) d -> p u d", p=P)).then_inc(ws_loaded, 16)
        for t in range(2, TQ):
            load_res(t)

        def load_w12(e):
            sp.dma_start(w12r[:, e, :, 0:HID], rw1[e].rearrange("(k p) h -> p k h", p=P)).then_inc(wr_loaded, 16)
            sp.dma_start(w12r[:, e, :, HID:], rw2[e].rearrange("(k p) h -> p k h", p=P)).then_inc(wr_loaded, 16)

        with sp.Fori(OVER_D, E) as e:
            load_w12(e)
        sp.wait_ge(o_turned, NT)
        with sp.Fori(0, E) as e:
            sp.dma_start(w3r[:, e, :, :], rw3[e].rearrange("(k p) d -> p k d", p=P)).then_inc(wr_loaded, 16)
        sp.wait_ge(gates_ready, 1)
        for e in range(OVER_D):
            load_w12(e)

        sp.wait_ge(scattered, 16 * NT * TOP)

        def slot(s, i, c):
            if inside(s + 3):
                wait(sp, slot_turned, s)
                sp.dma_start(xsl[:, (c + 3) % 4, :], xs_dram[bass.ds((s + 3) * P, P), :])\
                    .then_inc(slot_loaded[(c + 3) % 4], 16)
            if inside(s - 1):
                sp.wait_ge(yo_ready, s)
                sp.dma_start(ys_dram[bass.ds((s - 1) * P, P), :], yo[:, (c + 1) % 2, :])\
                    .then_inc(yo_stored[(c + 1) % 2], 16)

        for s in range(3):
            sp.dma_start(xsl[:, s, :], xs_dram[s * P:(s + 1) * P, :]).then_inc(slot_loaded[s], 16)
        slot_loop(sp, slot)

        for n in range(NT):
            sp.wait_ge(combined, n + 1)
            if n == 4 * GB:
                sp.wait_ge(ysh_added, NG)
            sp.dma_start(out[n % B, (n // B) * P:(n // B + 1) * P, :], x2[:, n, :]).then_inc(out_stored, 16)
        sp.wait_ge(out_stored, 16 * NT)

    @block.gpsimd
    def _(pool):
        g = nc.gpsimd
        g.memset(half[:, :, :], -0.5)
        g.memset(eps[:, :, :], LN_EPS)
        g.memset(ident[:, :], 0.0)
        g.drain()
        g.affine_select(out=ident[:, :], in_=ident[:, :], compare_op=ALU.not_equal, fill=1.0,
                        base=0, pattern=[[-1, P]], channel_multiplier=1)
        g.drain().then_inc(ident_made, 1)

        def deviations(made, count, ready):
            pool.wait_ge(made, count)
            g.tensor_tensor(sd[:, :, :], mv[:, :, 1:2], eps[:, :, :], ALU.add)
            g.drain()
            g.tensor_tensor(rs[:, :, :], sd[:, :, :], half[:, :, :], ALU.pow).then_inc(ready, 1)

        deviations(var_ready, 1, rs_ready)
        deviations(var_ready, 2, rs_ready)
        g.memset(firstrow[:, :].bitcast(F32), 0.0)
        for buf, value in ((maskf, MASKED), (zrow, 0.0), (zneg, 0.0), (own_tile, 0.0)):
            g.memset(buf[:, :], value)
        g.memset(zero[:, :], 0.0)
        g.memset(maskrow[:, :, :].bitcast(F32), 0.0)
        g.drain()

        def stage_a(t):
            deviations(var_ready, 2 * t + 3, rs_ready)
            if not (isinstance(t, int) and t == TQ - 1):
                deviations(var_ready, 2 * t + 4, rs_ready)

        stage_a(0)
        pool.wait_ge(consts_loaded, 16 * NC_CONST)
        for b in range(B):
            g.tensor_scalar(maskf[0:M, b * H:(b + 1) * H], mask_i[:, b:b + 1].to_broadcast([M, H]), -1.0, -MASKED,
                            ALU.add, ALU.mult)
        g.drain()
        for b in range(B):
            g.tensor_scalar(maskrow[0:1, b * H:(b + 1) * H, :], maskrow_i[:, b:b + 1, :].to_broadcast([1, H, M]),
                            -1.0, -MASKED, ALU.add, ALU.mult)
        g.memset(firstrow[0:1, :].bitcast(F32), 1.0)
        g.drain()
        g.tensor_scalar(qks[:, 0:1], qks[:, 0:1], SCALE, None, ALU.mult)
        g.affine_select(out=own_tile[:, :], in_=own_tile[:, :], compare_op=ALU.not_equal, fill=1.0,
                        base=-DH, pattern=[[-1, TQ]], channel_multiplier=1)
        g.drain().then_inc(masks_made, 1)
        with pool.Fori(1, TQ - 1) as t:
            stage_a(t)
        stage_a(TQ - 1)

        def collect(hh):
            pool.wait_ge(heads_turned, NTURN * hh)
            g.tensor_copy(tiles[:, 0:TK, :], kn[:, hh, :, :])
            g.tensor_copy(tiles[:, TK:TK + 1, :], kn[:, hh, TQ:TK, :])
            g.tensor_copy(tiles[:, TK + 1:, :], on[:, :, hh, :]).then_inc(collected, 1)

        with pool.Fori(1, BH) as hh:
            collect(hh)

        pool.wait_ge(o_ready, CH * BH)
        g.memset(upper[:, :], 1.0)
        g.memset(allones[:, :], 1.0)
        g.iota(number_i[:, :], pattern=[[1, E]], base=-int(FAR), channel_multiplier=0)
        g.iota(slot_i[:, :], pattern=[[1, NS + 1]], base=0, channel_multiplier=0)
        g.drain()
        g.tensor_copy(number[:, :], number_i[:, :])
        g.tensor_copy(slot_f[:, :], slot_i[:, :])
        g.affine_select(out=upper[:, :], in_=upper[:, :], compare_op=ALU.is_gt, fill=0.0,
                        base=0, pattern=[[1, P]], channel_multiplier=-1)
        g.drain().then_inc(d_consts, 1)

        pool.wait_ge(c_loaded, 64)

        def add_bias(t):
            pool.wait_ge(xres_loaded[t % 2], 32 * (t // 2 + 1))
            g.tensor_tensor(xres[:, t % 2, :, :], xres[:, t % 2, :, :], lno[:, 1, :].unsqueeze(1).to_broadcast([P, 2, D]),
                            ALU.add).then_inc(xres_ready, 1)

        add_bias(0)
        add_bias(1)
        for t in range(TQ):
            for k in range(2):
                deviations(cvar_ready, 2 * t + k + 1, crs_ready)
            if t + 2 < TQ:
                add_bias(t + 2)

        pool.wait_ge(placed, 1)
        pool.wait_ge(xs_zeroed, 16 * NS)
        for n in range(NT):
            for k in range(TOP):
                g.indirect_dma_start(out=xs_dram, out_offset=bass.IndirectOffsetOnAxis(ap=posi[:, n, k:k + 1], axis=0),
                                     in_=xf[:, n, :], in_offset=None).then_inc(scattered, 16)

        for p in range(2):
            pool.wait_ge(yo_stored[p], 16 * ((NS + 1 - p) // 2))
        for n in range(NT):
            wait(pool, combined, n - NGAT + 1)
            for k in range(TOP):
                g.indirect_dma_start(out=gat[n % NGAT][:, k, :], out_offset=None, in_=ys_dram,
                                     in_offset=bass.IndirectOffsetOnAxis(ap=posi[:, n, k:k + 1], axis=0)
                                     ).then_inc(gathered[n % NGAT], 16)

    @block.tensor
    def _(pe):
        mm_ = nc.tensor.matmul
        pe.wait_ge(ident_made, 1)

        def turn_x(t):
            pe.wait_ge(xnorm_ready, t + 1)
            for c in range(B):
                for k in range(DK):
                    last = nc.tensor.transpose(bank[c][:, k * P:(k + 1) * P], xn2[:, c, k * P:(k + 1) * P], ident[:, :])
                last.then_inc(xt_turned, 1)

        def project(n, c, j):
            made, used = ((q_made, q_used), (k_made, k_used), (v_made, v_used))[j]
            pe.wait_ge(xT_ready, n + 1)
            wait(pe, used, n - 1)
            for k in range(DK):
                last = mm_(bank[2 + 3 * c + j][:, :], xT[:, c, k, :], wqkv[:, k, j * INNER:(j + 1) * INNER],
                           start=(k == 0), stop=(k == DK - 1))
            last.then_inc(made, 1)

        turn_x(0)

        def stage_a(t):
            for j in range(3):
                project(2 * t, 0, j)
            for j in range(2):
                project(2 * t + 1, 1, j)
            turn_x(t + 1)
            project(2 * t + 1, 1, 2)

        pe.wait_ge(w_loaded, 16 * 2 * DK)
        pair_loop(pe, stage_a, TQ)
        for c in range(B):
            for j in (1, 2):
                project(NT + c, c, j)

        pe.wait_ge(q_used, NT)
        pe.wait_ge(k_used, NT + B)
        pe.wait_ge(v_used, NT + B)
        pe.wait_ge(masks_made, 1)
        pe.wait_ge(consts_made, 1)

        def turn_head(hh, g):
            what, first, n, b = TURNS[g]
            if what == "k":
                pe.wait_ge(collected, hh + 1)
                wait(pe, split, len(PARTS) * hh)
            elif what == "q":
                wait(pe, neg_row, 2 * hh)
            else:
                pe.wait_ge(split, part(hh, "k odd"))
            for j in range(n):
                pair = tiles[:, first + 2 * j:first + 2 * j + 2, :].rearrange("p a d -> p (a d)")
                last = nc.tensor.transpose(bank[b][:, j * P:(j + 1) * P], pair, ident[:, :])
            last.then_inc(heads_turned, 1)

        def piece(hh, p, k, banks=(2, 3)):
            tile, c = divmod(k, len(PIECES))
            first, n = PIECES[c]
            if k == 0:
                pe.wait_ge(split, part(hh, "q even"))
            elif c == 2 and tile == 0:
                pe.wait_ge(split, part(hh, "ctx"))
            wait(pe, piece_used, NP_ * hh + k + 1 - len(banks))
            dst = bank[banks[k % len(banks)]]
            last = mm_(dst[:, 0:n], qT1[p][:, tile * P:(tile + 1) * P], kT1[p][:, first:first + n],
                       start=True, stop=(c < 2))
            if c == 2:
                last = mm_(dst[:, n - M:n], firstrow[:, :], maskrow[:, hh, :], start=False, stop=True)
            last.then_inc(piece_made, 1)

        def turn_neg(hh):
            pe.wait_ge(neg_ready, hh + 1)
            nc.tensor.transpose(bank[NEG_BANK][0:DH + TQ, 0:P], zneg[:, :], ident[:, :]).then_inc(neg_turned, 1)

        def score_tile(hh, p, s):
            c, kt = divmod(s, TK)
            if s == 0:
                pe.wait_ge(neg_row, 2 * hh + 1)
            if s == TK:
                pe.wait_ge(neg_row, 2 * hh + 2)
            wait(pe, probs_ready, STEPS * hh + s - 1)
            mm_(bank[s % 2][:, :], kT1[p][:, kt * P:(kt + 1) * P], qT1[p][:, c * QC:(c + 1) * QC],
                start=True, stop=False)
            mm_(bank[s % 2][:, :], kT2[p][:, kt * P:(kt + 1) * P], qT2[p][:, c * QC:(c + 1) * QC],
                start=False, stop=True).then_inc(scores_made, 1)

        def weigh(hh, s, between=()):
            c, kt = divmod(s, TK)
            between = list(between)
            for j in range(QC // P):
                if j % 2 == 0 and between:
                    between.pop(0)()
                if j == 0:
                    pe.wait_ge(probs_ready, STEPS * hh + s + 1)
                    if kt == 0:
                        wait(pe, o_ready, CH * hh + c - 1)
                last = mm_(bank[4 + c][:, j * (DH + 1):(j + 1) * (DH + 1)], prob[:, s % 3, j * P:(j + 1) * P],
                           vn[:, hh, kt, :], start=(kt == 0 and j == 0), stop=(kt == TK - 1),
                           skip_group_check=True)
            last.then_inc(pv_done, 1)
            for step in between:
                step()

        for g in range(NTURN):
            turn_head(0, g)
        for k in range(NP_):
            piece(0, 0, k, PREPARE_BANKS)
        turn_neg(0)

        def stage_b(hh, p, prepare):
            for s in range(STEPS):
                score_tile(hh, p, s)
                if prepare and s in TURN_AT:
                    turn_head(hh + 1, TURN_AT[s])
                if prepare and s == STEPS - 1:
                    turn_neg(hh + 1)
                pieces = piece_steps.get(s, ()) if prepare else ()
                if s >= 2:
                    weigh(hh, s - 2, pieces and [lambda k=k: piece(hh + 1, 1 - p, k) for k in pieces])
                elif not (isinstance(hh, int) and hh == 0):
                    weigh(hh - 1, STEPS + s - 2)

        head_loop(pe, stage_b)
        for s in (STEPS - 2, STEPS - 1):
            weigh(BH - 1, s)

        pe.wait_ge(o_ready, CH * BH)
        pe.wait_ge(c_loaded, 64)

        def turn_o(t, half=(0, 1)):
            for c, free in [((1, xf_moved), (0, logits_ready))[i] for i in half]:
                if t > EARLY:
                    wait(pe, free, t)
                for j in range(4):
                    src = on[:, t, c * H + 2 * j:c * H + 2 * j + 2, :].rearrange("p a d -> p (a d)")
                    last = nc.tensor.transpose(cbanks(t)[c][:, j * P:(j + 1) * P], src, ident[:, :])
                last.then_inc(o_turned, 1)

        def project_o(t):
            pe.wait_ge(oT_ready, 2 * t + 2)
            for c in range(B):
                for j in range(4):
                    last = mm_(cbanks(t)[0][:, c * D:(c + 1) * D], oT[:, t % 2, c, j * P:(j + 1) * P], wo_sb[:, j, :],
                               start=(c == 0 and j == 0), stop=(j == 3), skip_group_check=True)
            last.then_inc(y_made, 1)

        def turn_xf(t):
            pe.wait_ge(xf_ready, t + 1)
            if t == EARLY:
                pe.wait_ge(logits_ready, t)
            for c in range(B):
                for k in range(DK):
                    last = nc.tensor.transpose(cbanks(t, True)[1][:, (c * DK + k) * P:(c * DK + k + 1) * P],
                                               xf[:, 2 * t + c, k * P:(k + 1) * P], ident[:, :])
            last.then_inc(xf_turned, 1)

        def route(t):
            pe.wait_ge(xf_moved, t + 1)
            pe.wait_ge(y_used, t + 1)
            for k in range(DK):
                last = mm_(cbanks(t, True)[0][0:E, 0:B * P], wr[:, k, :], xfT[:, k, 2 * t * P:(2 * t + 2) * P],
                           start=(k == 0), stop=(k == DK - 1))
            last.then_inc(logits_made, 1)

        def turn_logits():
            pe.wait_ge(logits_ready, TQ)
            for n in range(NT):
                last = nc.tensor.transpose(bank[6][:, n * E:(n + 1) * E], logits[:, n * P:(n + 1) * P],
                                           ident[0:E, 0:E])
            last.then_inc(logits_turned, 1)

        turn_o(0)
        for t in range(FIRST + 1):
            if t < FIRST:
                turn_o(t + 1)
            project_o(t)
        for t in range(FIRST):
            turn_xf(t)
            route(t)

        def count_tokens():
            pe.wait_ge(taken_ready, 1)
            pe.wait_ge(d_consts, 1)
            pe.wait_ge(score_ready, 1)
            mm_(bank[6][:, 0:E], upper[:, :], taken[:, :], start=True, stop=True)
            mm_(bank[7][:, 0:E], allones[:, :], taken[:, :], start=True, stop=True).then_inc(counts_made, 1)

        def hidden(g, u, beside_pair=None):
            n = SU * g + u
            wait(pe, hid_ready, n - 1)
            for w in range(2):
                if w and beside_pair is not None:
                    turn_o(beside_pair, (1,))
                for k in range(DK):
                    last = mm_(bank[2 * (u % 2) + w][:, :], w12s[:, k, w, u * P:(u + 1) * P],
                               xfT[:, k, bass.ds(g * GR, GR)], start=(k == 0), stop=(k == DK - 1))
            last.then_inc(hid_made, 1)

        def down(g, u, beside_pair=None):
            pe.wait_ge(hid_ready, SU * g + u + 1)
            if u == 0:
                wait(pe, ysh_added, g)
            for j in range(4):
                if j == 2 and beside_pair is not None:
                    turn_xf(beside_pair)
                last = mm_(bank[4 + j // 2][:, (j % 2) * D:(j % 2 + 1) * D], gsh[:, u % 2, j * P:(j + 1) * P],
                           w3s[:, u, :], start=(u == 0 and j % 2 == 0), stop=(u == SU - 1), skip_group_check=True)
            if u == SU - 1:
                last.then_inc(ysh_made, 1)

        def shared(g):
            pe.wait_ge(xf_moved, 2 * g + 2)
            for u in range(SU):
                n = SU * g + u
                now, last = beside(n), beside(n - 2)
                if last is not None:
                    route(last)
                    if last == TQ - 1:
                        turn_logits()
                if now is not None and now <= EARLY:
                    now = None
                if now is not None:
                    turn_o(now, (0,))
                if n == 1:
                    pe.wait_ge(y_used, EARLY + 1)
                if n == COUNT_AT:
                    count_tokens()
                hidden(g, u, now)
                if now is not None:
                    project_o(now)
                if u:
                    down(g, u - 1, beside(n - 1))
            down(g, SU - 1)

        pe.wait_ge(ws_loaded, 48)
        for g in range(GB):
            shared(g)

        pe.wait_ge(wr_loaded, 16 * 3 * E)
        pe.wait_ge(routed, 1)

        def turn_slot(s, i, c):
            pe.wait_ge(slot_loaded[c % 4], 16 * (i + c // 4 + 1))
            for k in range(DK):
                last = nc.tensor.transpose(bank[c % 2][:, k * P:(k + 1) * P], xsl[:, c % 4, k * P:(k + 1) * P],
                                           ident[:, :])
            last.then_inc(slot_turned, 1)

        def slot_hidden(s, p):
            pe.wait_ge(slotT_ready, s + 1)
            pe.wait_ge(w_placed, s + 1)
            wait(pe, rg_ready, s - 1)
            for j in range(2 * HID // P):
                for k in range(DK):
                    last = mm_(bank[2 + p][:, j * P:(j + 1) * P], w_slot[:, p, k, j * P:(j + 1) * P], xsT[:, p, k, :],
                               start=(k == 0), stop=(k == DK - 1))
            last.then_inc(rh_made, 1)

        def slot_down(s, p):
            e = nc.tensor.value_load(exps[0:1, bass.ds(s, 1)], min_val=0, max_val=E - 1)
            pe.wait_ge(rg_ready, s + 1)
            wait(pe, yo_ready, s - 1)
            for k in range(HID // P):
                last = mm_(bank[6 + p][:, 0:D], rgT[:, p, k * P:(k + 1) * P], w3r[:, e, k, :],
                           start=(k == 0), stop=(k == HID // P - 1))
            last.then_inc(ry_made, 1)

        def slot(s, i, c):
            if inside(s):
                slot_hidden(s, c % 2)
            if inside(s + 1):
                turn_slot(s + 1, i, c + 1)
            if inside(s - 1):
                slot_down(s - 1, (c + 1) % 2)

        turn_slot(0, 0, 0)
        slot_loop(pe, slot)

        for g in range(GB, NG):
            shared(g)

    @block.scalar
    def _(act):
        a = nc.scalar.activation
        for kind, vecs in enumerate(((ln_l_w, ln_l_b), (ln_x_w, ln_x_b))):
            for i, vec in enumerate(vecs):
                for k in range(DK):
                    act.dma_start(lnw[:, kind, i, k:k + 1],
                                  vec[k * P:(k + 1) * P].rearrange("(p a) -> p a", a=1)).then_inc(ln_loaded, 16)

        def affine(n, c, kind):
            act.wait_ge(xt_turned, n + 1)
            wait(act, v_made, n - 1)
            for k in range(DK):
                last = a(xT[:, c, k, :], bank[c][:, k * P:(k + 1) * P], ACT.Identity,
                         scale=lnw[:, kind, 0, k:k + 1], bias=lnw[:, kind, 1, k:k + 1])
            last.then_inc(xT_ready, 1)

        def square(n, c, i):
            wait(act, ssq_ready, n)
            act.wait_ge((q_made, k_made)[i], n + 1)
            a(sq[:, i, :], bank[2 + 3 * c + i][:, :], ACT.Square).then_inc(sq_ready, 1)

        def keep_v(t, n, c):
            act.wait_ge(v_made, n + 1)
            a(vn[:, c * H:(c + 1) * H, t, 0:DH], bank[4 + 3 * c][:, :].rearrange("p (h d) -> p h d", d=DH),
              ACT.Copy).then_inc(v_used, 1)

        def lengths(n):
            act.wait_ge(ssq_ready, n + 1)
            a(nrm[:, :], ssq[:, :], ACT.Sqrt).then_inc(nrm_ready, 1)

        act.wait_ge(ln_loaded, 16 * 4 * DK)
        for c in range(B):
            affine(c, c, 0)

        def stage_a(t):
            last = isinstance(t, int) and t == TQ - 1
            if not (isinstance(t, int) and t == 0):
                lengths(2 * t - 1)
            square(2 * t, 0, 0)
            square(2 * t, 0, 1)
            keep_v(t, 2 * t, 0)
            lengths(2 * t)
            square(2 * t + 1, 1, 0)
            square(2 * t + 1, 1, 1)
            for c in range(B):
                affine(2 * t + 2 + c, c, 1 if last else 0)
            keep_v(t, 2 * t + 1, 1)

        pair_loop(act, stage_a, TQ)
        lengths(NT - 1)
        for c in range(B):
            square(NT + c, c, 1)
            keep_v(TQ, NT + c, c)
            lengths(NT + c)

        act.wait_ge(masks_made, 1)
        act.wait_ge(consts_made, 1)
        act.wait_ge(k_used, NT + B)

        def round_part(hh, p, what):
            if what == "ctx":
                act.wait_ge(heads_turned, NTURN * hh + 3)
                last = a(kT1[p][:, TQ * P:], bank[6][:, 0:P], ACT.Copy, scale=qks[:, 1:2])
            elif what[0] == "k":
                odd = what == "k odd"
                rows = HIGH if odd else LOW
                act.wait_ge(heads_turned, NTURN * hh + 1)
                for dst in (LOW, HIGH):
                    last = a(tiles_of(kT1[p], dst, odd), turned(6, rows), ACT.Copy, scale=qks[rows, 1:2])
            else:
                odd = what == "q odd"
                rows = HIGH if odd else LOW
                act.wait_ge(heads_turned, NTURN * hh + 2)
                a(tiles_of(qT1[p], rows, odd), turned(7, rows), ACT.Copy, scale=qks[rows, 0:1])
                last = a(tiles_of(qT2[p], LOW, odd), turned(7, rows), ACT.Copy, scale=qks[rows, 0:1])
            last.then_inc(scaled, 1)

        def exponentials(hh, p, s):
            act.wait_ge(scores_made, STEPS * hh + s + 1)
            wait(act, pv_done, STEPS * hh + s - 2)
            bias = mbias[p][:, :] if s % TK == TK - 1 else zero[:, :]
            a(prob[:, s % 3, :], bank[s % 2][:, :], ACT.Exp, bias=bias).then_inc(probs_ready, 1)

        for what in PARTS:
            round_part(0, 0, what)

        def stage_b(hh, p, prepare):
            for s in range(STEPS):
                exponentials(hh, p, s)
                if prepare:
                    if s in ROUND_AT:
                        round_part(hh + 1, 1 - p, ROUND_AT[s])

        head_loop(act, stage_b)


        def copy_oT(t):
            wait(act, y_made, t - 1)
            for i, c in enumerate((1, 0)):
                act.wait_ge(o_turned, 2 * t + i + 1)
                a(oT[:, t % 2, c, :], cbanks(t)[c][:, :], ACT.Copy).then_inc(oT_ready, 1)

        def copy_xfT(t):
            act.wait_ge(xf_turned, t + 1)
            src = cbanks(t, True)[1][:, :].rearrange("p (c k n) -> p k c n", c=B, k=DK)
            dst = xfT[:, :, 2 * t * P:(2 * t + 2) * P].rearrange("p k (c n) -> p k c n", c=B)
            a(dst, src, ACT.Copy).then_inc(xf_moved, 1)

        def copy_logits(t):
            act.wait_ge(logits_made, t + 1)
            a(logits[:, 2 * t * P:(2 * t + 2) * P], cbanks(t, True)[0][0:E, 0:B * P], ACT.Copy).then_inc(logits_ready, 1)

        for t in range(FIRST + 1):
            copy_oT(t)
        for t in range(FIRST):
            copy_xfT(t)
            copy_logits(t)

        def shared(g):
            for u in range(SU):
                n = SU * g + u
                now, last = beside(n), beside(n - 2)
                if last is not None:
                    copy_logits(last)
                    if last == TQ - 1:
                        act.wait_ge(logits_turned, 1)
                        a(score[:, :, :], bank[6][:, 0:NT * E].rearrange("p (n e) -> p n e", e=E),
                          ACT.Sigmoid).then_inc(score_ready, 1)
                if now is not None and now > EARLY:
                    copy_oT(now)
                act.wait_ge(hid_made, n + 1)
                wait(act, hid_ready, n - 1)
                a(sil[:, u % 2, :], bank[2 * (u % 2)][:, :], ACT.Silu).then_inc(sil_ready, 1)
                if beside(n - 1) is not None:
                    copy_xfT(beside(n - 1))

        for g in range(GB):
            shared(g)

        def copy_slotT(s, p):
            act.wait_ge(slot_turned, s + 1)
            a(xsT[:, p, :, :], bank[p][:, 0:D].rearrange("p (k n) -> p k n", k=DK), ACT.Copy).then_inc(slotT_ready, 1)

        def slot_silu(s, p):
            act.wait_ge(rh_made, s + 1)
            wait(act, rg_ready, s - 1)
            a(sil[:, p, 0:HID], bank[2 + p][:, 0:HID], ACT.Silu).then_inc(rsil_ready, 1)

        def copy_result(s, p, before):
            act.wait_ge(ry_made, s + 1)
            wait(act, yo_stored[p], 16 * before)
            a(yo[:, p, :], bank[6 + p][:, 0:D], ACT.Copy).then_inc(yo_ready, 1)

        def slot(s, i, c):
            if inside(s):
                slot_silu(s, c % 2)
            if inside(s + 1):
                copy_slotT(s + 1, (c + 1) % 2)
            if inside(s - 1):
                copy_result(s - 1, (c + 1) % 2, 2 * i + (c - 1) // 2)

        copy_slotT(0, 0)
        slot_loop(act, slot)

        for g in range(GB, NG):
            shared(g)

    @block.vector
    def _(dve):
        v = nc.vector

        def variances(src, ready):
            for c in range(B):
                v.bn_stats(st[:, c, :], src(c))
            v.drain()
            for c in range(B):
                last = v.bn_aggr(mv[:, c, :], st[:, c, :])
            last.then_inc(ready, 1)
            v.drain()

        def normalise(dst, src, done):
            for c in range(B):
                last = v.tensor_scalar(dst(c), src(c), mv[:, c, 0:1], rs[:, c, :], ALU.subtract, ALU.mult)
            last.then_inc(done, 1)

        def sum_squares(n, latent, sq_at):
            for j, i in enumerate((0, 1) if latent else (1,)):
                dve.wait_ge(sq_ready, sq_at + j + 1)
                last = v.tensor_reduce(ssq[:, i * H:(i + 1) * H], sq[:, i, :].rearrange("p (h d) -> p h d", d=DH),
                                       AX.X, ALU.add)
            last.then_inc(ssq_ready, 1)

        def divide_qk(t, n, c, latent):
            dve.wait_ge(nrm_ready, n + 1)
            v.tensor_scalar(rnr[:, :], nrm[:, :], L2_EPS, None, ALU.max)
            v.drain()
            v.reciprocal(rnr[:, :], rnr[:, :])
            v.drain()
            for i, used, dst in ((0, q_used, on), (1, k_used, kn)) if latent else ((1, k_used, kn),):
                rows = dst[:, t, c * H:(c + 1) * H, :] if i == 0 else dst[:, c * H:(c + 1) * H, t, :]
                v.tensor_tensor(rows, bank[2 + 3 * c + i][:, :].rearrange("p (h d) -> p h d", d=DH),
                                rnr[:, i * H:(i + 1) * H].unsqueeze(2).to_broadcast([P, H, DH]),
                                ALU.mult).then_inc(used, 1)

        xin_, xn_, xn2_ = (lambda c: xin[:, c, :]), (lambda c: xn[:, c, :]), (lambda c: xn2[:, c, :])
        dve.wait_ge(x_loaded, 32)
        variances(xin_, var_ready)
        dve.wait_ge(rs_ready, 1)
        normalise(xn_, xin_, x_used)
        v.drain()
        variances(xn_, var_ready)
        dve.wait_ge(rs_ready, 2)
        normalise(xn2_, xn_, xnorm_ready)
        v.memset(vn[:, :, :, DH:DH + 1], 1.0)
        for i in range(2):
            v.memset(qT2[i][DH:P, :].bitcast(F32), 0.0)
            v.memset(kT2[i][DH:P, :].bitcast(F32), 0.0)
        v.drain()
        for i in range(2):
            last = v.memset(kT2[i][DH:DH + TQ, :].bitcast(F32), 1.0)
        last.then_inc(consts_made, 1)

        def stage_a(t):
            begun = not (isinstance(t, int) and t == 0)
            context = isinstance(t, int) and t == TQ - 1
            if begun:
                sum_squares(2 * t - 1, True, 2 * (2 * t - 1))
            dve.wait_ge(x_loaded, 32 * (t + 2) + (32 if context else 0))
            variances(xin_, var_ready)
            if begun:
                divide_qk(t - 1, 2 * t - 1, 1, True)
            if not context:
                dve.wait_ge(rs_ready, 2 * t + 3)
                normalise(xn_, xin_, x_used)
                v.drain()
                variances(xn_, var_ready)
            sum_squares(2 * t, True, 2 * (2 * t))
            dve.wait_ge(rs_ready, 2 * t + (3 if context else 4))
            dve.wait_ge(xt_turned, 2 * t + 2)
            normalise(xn2_, xin_ if context else xn_, xnorm_ready)
            divide_qk(t, 2 * t, 0, True)

        pair_loop(dve, stage_a, TQ)
        sum_squares(NT - 1, True, 2 * (NT - 1))
        divide_qk(TQ - 1, NT - 1, 1, True)
        for c in range(B):
            sum_squares(NT + c, False, 2 * NT + c)
            divide_qk(TQ, NT + c, c, False)
        v.drain()

        dve.wait_ge(masks_made, 1)

        def split_part(hh, p, what):
            dve.wait_ge(scaled, part(hh, what))
            if what == "ctx":
                v.scalar_tensor_tensor(kT2[p][LOW, TQ * P:], bank[6][LOW, 0:P], qks[LOW, 1:2], kT1[p][LOW, TQ * P:],
                                       ALU.mult, ALU.subtract).then_inc(split, 1)
                return
            odd = what.endswith("odd")
            rows = HIGH if odd else LOW
            if what[0] == "k":
                out_, src, scale, hi = tiles_of(kT2[p], LOW, odd), turned(6, rows), qks[rows, 1:2], kT1[p]
            else:
                out_, src, scale, hi = tiles_of(qT1[p], LOW if odd else HIGH, odd), turned(7, rows), qks[rows, 0:1], qT1[p]
            v.scalar_tensor_tensor(out_, src, scale, tiles_of(hi, rows, odd), ALU.mult, ALU.subtract).then_inc(split, 1)

        def reduce_piece(hh, k, banks=(2, 3)):
            tile, c = divmod(k, len(PIECES))
            dve.wait_ge(piece_made, NP_ * hh + k + 1)
            v.tensor_reduce(mx[:, tile, c:c + 1], bank[banks[k % len(banks)]][:, 0:PIECES[c][1]], AX.X, ALU.max)\
                .then_inc(piece_used, 1)

        def negate(hh, p):
            v.tensor_scalar(mbias[p][:, :], maskf[:, bass.ds(hh, 1)], 0.0, None, ALU.add)
            v.drain()
            v.tensor_reduce(mm[:, :], mx[:, :, :], AX.X, ALU.max)
            v.drain()
            wait(dve, neg_turned, hh)
            v.tensor_scalar(zneg[:, DH:], mm[:, :], -1.0, None, ALU.mult).then_inc(neg_ready, 1)

        def keep_neg(hh, p):
            dve.wait_ge(neg_turned, hh + 1)
            rows = slice(DH, DH + TQ)
            for z in range(CH):
                n = TQ // CH
                v.tensor_tensor(qT2[p][rows, z * QC:(z + 1) * QC].rearrange("p (t c) -> p t c", c=P),
                                bank[NEG_BANK][rows, 0:P].unsqueeze(1).to_broadcast([TQ, n, P]),
                                own_tile[rows, z * n:(z + 1) * n].unsqueeze(2).to_broadcast([TQ, n, P]),
                                ALU.mult).then_inc(neg_row, 1)

        def divide(hh, c):
            dve.wait_ge(pv_done, STEPS * hh + TK * (c + 1))
            sums = bank[4 + c][:, 0:4 * (DH + 1)].rearrange("p (j d) -> p j d", d=DH + 1)
            v.reciprocal(rec[:, c, :], sums[:, :, DH])
            v.drain()
            v.tensor_tensor(on[:, 4 * c:4 * c + 4, hh, :], sums[:, :, 0:DH],
                            rec[:, c, :].unsqueeze(2).to_broadcast([P, 4, DH]), ALU.mult).then_inc(o_ready, 1)

        v.tensor_copy(tiles[:, 0:TK, :], kn[:, 0, :, :])
        v.tensor_copy(tiles[:, TK:TK + 1, :], kn[:, 0, TQ:TK, :])
        v.tensor_copy(tiles[:, TK + 1:, :], on[:, :, 0, :]).then_inc(collected, 1)
        for what in PARTS:
            split_part(0, 0, what)
        for k in range(NP_):
            reduce_piece(0, k, PREPARE_BANKS)
        negate(0, 0)
        keep_neg(0, 0)

        def stage_b(hh, p, prepare):
            for s in range(STEPS):
                if prepare:
                    for what in REST_AT.get(s, ()):
                        split_part(hh + 1, 1 - p, what)
                    for k in piece_steps.get(s, ()):
                        reduce_piece(hh + 1, k)
                if s == 2 and not (isinstance(hh, int) and hh == 0):
                    divide(hh - 1, 1)
                if s == TK + 2:
                    divide(hh, 0)
            if prepare:
                negate(hh + 1, 1 - p)
                keep_neg(hh + 1, 1 - p)

        head_loop(dve, stage_b)
        divide(BH - 1, 1)

        v.drain()
        dve.wait_ge(c_loaded, 64)

        def product(g, u):
            n = SU * g + u
            dve.wait_ge(sil_ready, n + 1)
            v.tensor_tensor(gsh[:, u % 2, :], sil[:, u % 2, :], bank[2 * (u % 2) + 1][:, :], ALU.mult).then_inc(hid_ready, 1)

        def add_shared(g):
            dve.wait_ge(ysh_made, g + 1)
            for j in range(2):
                rows = x2[:, 4 * g + 2 * j:4 * g + 2 * j + 2, :]
                last = v.tensor_tensor(rows, bank[4 + j][:, :].rearrange("p (c d) -> p c d", c=2), rows, ALU.add)
            last.then_inc(ysh_added, 1)
            v.drain()

        def stage_c(t):
            y = lambda c: cbanks(t)[0][:, c * D:(c + 1) * D]
            dve.wait_ge(y_made, t + 1)
            variances(y, cvar_ready)
            for c in range(B):
                last = v.scalar_tensor_tensor(yn[:, c, :], y(c), mv[:, c, 0:1], lno[:, 0, :], ALU.subtract, ALU.mult)
            last.then_inc(y_used, 1)
            v.drain()
            dve.wait_ge(xres_ready, t + 1)
            dve.wait_ge(crs_ready, 2 * t + 1)
            for c in range(B):
                last = v.scalar_tensor_tensor(x2[:, 2 * t + c, :], yn[:, c, :], rs[:, c, :], xres[:, t % 2, c, :],
                                              ALU.mult, ALU.add)
            last.then_inc(xres_used, 1)
            v.drain()
            x2_ = lambda c: x2[:, 2 * t + c, :]
            variances(x2_, cvar_ready)
            dve.wait_ge(crs_ready, 2 * t + 2)
            normalise(lambda c: xf[:, 2 * t + c, :], x2_, xf_ready)

        for t in range(FIRST + 1):
            stage_c(t)
        hid = 0

        def shared_product():
            nonlocal hid
            if hid % SU == 0 and hid:
                add_shared(hid // SU - 1)
            product(hid // SU, hid % SU)
            hid += 1

        while beside(hid) is not None:
            shared_product()
            if beside(hid - 1) > EARLY:
                stage_c(beside(hid - 1))
            shared_product()

        dve.wait_ge(score_ready, 1)
        dve.wait_ge(d_consts, 1)

        def over_tiles(ap):
            return ap.unsqueeze(1).to_broadcast([P, NT, E])

        def over_experts(ap):
            return ap.unsqueeze(2).to_broadcast([P, NT, E])

        v.tensor_tensor(sel[:, :, :], score[:, :, :], over_tiles(ebias[:, :]), ALU.add)
        v.drain()
        for k in range(TOP):
            v.tensor_reduce(best[:, :], sel[:, :, :], AX.X, ALU.max)
            v.drain()
            v.tensor_tensor(work[0][:, :, :], sel[:, :, :], over_experts(best[:, :]), ALU.is_equal)
            v.drain()
            v.tensor_tensor(work[0][:, :, :], work[0][:, :, :], over_tiles(number[:, :]), ALU.mult)
            v.drain()
            shared_product()
            v.tensor_reduce(best[:, :], work[0][:, :, :], AX.X, ALU.min)
            v.drain()
            v.tensor_tensor(onehot[k][:, :, :], over_tiles(number[:, :]), over_experts(best[:, :]), ALU.is_equal)
            v.drain()
            if k < TOP - 1:
                v.scalar_tensor_tensor(sel[:, :, :], onehot[k][:, :, :], MASKED, sel[:, :, :], ALU.mult, ALU.add)
                v.drain()
        v.tensor_tensor(work[0][:, :, :], onehot[0][:, :, :], onehot[1][:, :, :], ALU.add)
        v.drain()
        v.tensor_reduce(taken[:, :], work[0][:, :, :].rearrange("p n e -> p e n"), AX.X, ALU.add).then_inc(taken_ready, 1)
        v.memset(work[1][:, 0:1, :], 0.0)
        v.tensor_copy(work[1][:, 1:NT, :], work[0][:, 0:NT - 1, :])
        v.drain()
        src, step = 1, 1
        while step < NT:
            v.tensor_copy(work[1 - src][:, 0:step, :], work[src][:, 0:step, :])
            v.tensor_tensor(work[1 - src][:, step:NT, :], work[src][:, step:NT, :], work[src][:, 0:NT - step, :], ALU.add)
            v.drain()
            src, step = 1 - src, 2 * step
        before = work[src]
        shared_product()
        dve.wait_ge(counts_made, 1)
        v.tensor_scalar(tiles_f[:, :], bank[7][:, 0:E], float(P - 1), None, ALU.add)
        v.drain()
        v.tensor_copy(tiles_i[:, :], tiles_f[:, :])
        v.drain()
        v.tensor_scalar(tiles_i[:, :], tiles_i[:, :], P.bit_length() - 1, None, ALU.logical_shift_right)
        v.drain()
        v.tensor_copy(tiles_f[:, :], tiles_i[:, :])
        v.drain()
        v.tensor_copy(ends[0][:, :], tiles_f[:, :])
        v.drain()
        src, step = 0, 1
        while step < E:
            v.tensor_copy(ends[1 - src][:, 0:step], ends[src][:, 0:step])
            v.tensor_tensor(ends[1 - src][:, step:E], ends[src][:, step:E], ends[src][:, 0:E - step], ALU.add)
            v.drain()
            src, step = 1 - src, 2 * step
        end = ends[src]
        shared_product()
        v.tensor_tensor(offs[:, :], end[:, :], tiles_f[:, :], ALU.subtract)
        v.drain()
        v.tensor_scalar(offs[:, :], offs[:, :], float(P), None, ALU.mult)
        v.drain()
        v.tensor_tensor(offs[:, :], offs[:, :], bank[6][:, 0:E], ALU.add)
        v.drain()
        v.tensor_tensor(before[:, :, :], before[:, :, :], over_tiles(offs[:, :]), ALU.add)
        v.drain()
        for k in range(TOP):
            v.tensor_tensor(sel[:, :, :], onehot[k][:, :, :], before[:, :, :], ALU.mult)
            v.drain()
            v.tensor_reduce(posf[:, :], sel[:, :, :], AX.X, ALU.add)
            v.drain()
            v.tensor_copy(posi[:, :, k], posf[:, :])
            v.drain()
        v.drain().then_inc(placed, 1)
        shared_product()
        v.tensor_tensor(passed[:, :, :], end[0:1, :].unsqueeze(1).to_broadcast([1, NS + 1, E]),
                        slot_f[:, :].unsqueeze(2).to_broadcast([1, NS + 1, E]), ALU.is_le)
        v.drain()
        v.tensor_reduce(passed_sum[:, :], passed[:, :, :], AX.X, ALU.add)
        v.drain()
        v.tensor_scalar(passed_sum[:, :], passed_sum[:, :], float(E - 1), None, ALU.min)
        v.drain()
        v.tensor_copy(exps[0:1, :], passed_sum[:, :])
        v.drain().then_inc(routed, 1)
        shared_product()
        for k in range(TOP):
            v.tensor_tensor(work[0][:, :, :], onehot[k][:, :, :], score[:, :, :], ALU.mult)
            v.drain()
            v.tensor_reduce(gate[:, :, k], work[0][:, :, :], AX.X, ALU.add)
            v.drain()
        v.drain().then_inc(gates_ready, 1)

        while hid < SU * GB:
            shared_product()

        def place_weights(s, p):
            e = nc.vector.value_load(exps[0:1, bass.ds(s, 1)], min_val=0, max_val=E - 1)
            v.tensor_copy(w_slot[:, p, :, :], w12r[:, e, :, :]).then_inc(w_placed, 1)

        def slot_product(s, p):
            dve.wait_ge(rsil_ready, s + 1)
            wait(dve, ry_made, s - 1)
            v.tensor_tensor(rgT[:, p, :], sil[:, p, 0:HID], bank[2 + p][:, HID:], ALU.mult).then_inc(rg_ready, 1)

        def slot(s, i, c):
            if inside(s):
                slot_product(s, c % 2)
            if inside(s + 2):
                place_weights(s + 2, c % 2)

        dve.wait_ge(wr_loaded, 16 * 3 * E)
        place_weights(0, 0)
        place_weights(1, 1)
        add_shared(GB - 1)
        slot_loop(dve, slot)

        def combine(n):
            dve.wait_ge(gathered[n % NGAT], 32 * (n // NGAT + 1))
            for k in range(TOP):
                last = v.scalar_tensor_tensor(x2[:, n, :], gat[n % NGAT][:, k, :], gate[:, n, k:k + 1], x2[:, n, :],
                                              ALU.mult, ALU.add)
                if k < TOP - 1:
                    v.drain()
            last.then_inc(combined, 1)

        done = 0
        for u in range(SU):
            product(GB, u)
            while done < min(NT, (NT * (u + 1)) // SU - 1):
                combine(done)
                done += 1
        while done < NT:
            combine(done)
            done += 1
        v.drain()
        add_shared(GB)

    es.close()


_INS = ["x", "ctx_1024", "mask_BxS2_bk0", "L0_xattn_ln_x_w", "L0_xattn_ln_x_b", "L0_xattn_ln_l_w",
        "L0_xattn_ln_l_b", "L0_xattn_Wq", "L0_xattn_Wkv", "L0_xattn_q_scale", "L0_xattn_k_scale",
        "L0_xattn_Wo", "L0_xattn_ln_o_w", "L0_xattn_ln_o_b", "L0_ffn_router_w", "L0_ffn_expert_bias",
        "L0_ffn_shared_w1", "L0_ffn_shared_w2", "L0_ffn_shared_w3", "L0_ffn_routed_w1",
        "L0_ffn_routed_w2", "L0_ffn_routed_w3"]


def kernel(**inputs):
    import numpy as np
    import concourse.bacc as bacc
    from concourse.bass_utils import run_bass_kernel_spmd

    nc = bacc.Bacc("TRN2", target_bir_lowering=False, num_devices=1)
    arrays, args = {}, []
    for name in _INS:
        a = np.ascontiguousarray(inputs[name])
        if a.dtype == np.bool_:
            a = a.astype(np.int32)
        arrays[f"in_{name}"] = a
        args.append(nc.dram_tensor(f"in_{name}", a.shape, mybir.dt.from_np(a.dtype), kind="ExternalInput").ap())
    out = nc.dram_tensor("out", (B, S, D), F32, kind="ExternalOutput").ap()
    build(nc, *args, out)
    r = run_bass_kernel_spmd(nc, [arrays], core_ids=[0])
    return r.results[0]["out"]
```
